# Optimizing a Trainium2 kernel written in Bass

```python
import numpy as np
import jax
import jax.numpy as jnp

def _softmax(x, axis=-1):
    return jax.nn.softmax(x, axis=axis)

def _gelu(x):
    return jax.nn.gelu(x, approximate=True)

def _silu(x):
    return jax.nn.silu(x)

def _sigmoid(x):
    return jax.nn.sigmoid(x)

def _layernorm(x, axis=-1, eps=1e-05):
    m = jnp.mean(x, axis=axis, keepdims=True)
    v = jnp.var(x, axis=axis, keepdims=True)
    return (x - m) / jnp.sqrt(v + eps)

def _scatter_add(tgt, idx, src, axis=0):
    return tgt.at[idx].add(src)

def _segment_sum(src, seg, n):
    return jax.ops.segment_sum(src, seg, n)
kernel_name = 'mk_xattn_seq_d1_seqx_r8_dbba2e'

def setup_inputs(seed: int=0):
    np.random.seed(seed)
    _w = jnp.asarray

    def _rec_inputs():
        import jax
        import jax.numpy as jnp
        _rk = jax.random.key(seed)
        x = -0.0005207 + 1.001 * jax.random.normal(jax.random.fold_in(_rk, 1), (2, 256, 128), jnp.float32)
        _lenS = 256 - jax.random.randint(jax.random.fold_in(_rk, 7), (2,), 0, max(1, 256 // 4) + 1, jnp.int32)
        _lenS2 = 512 - jax.random.randint(jax.random.fold_in(_rk, 8), (2,), 0, max(1, 512 // 4) + 1, jnp.int32)
        _ctx_1024P = jax.random.normal(jax.random.fold_in(_rk, 11), (2, 16, 128), jnp.float32)
        _ctx_1024c = jax.random.dirichlet(jax.random.fold_in(_rk, 511), 0.3 * jnp.ones((16,), jnp.float32), (2, 512))
        _ctx_1024t = jnp.einsum('bsk,bkd->bsd', _ctx_1024c, _ctx_1024P)
        _ctx_1024t = _ctx_1024t * jax.lax.rsqrt(jnp.mean(jnp.square(_ctx_1024t)) + 1e-12) * 0.953939
        ctx_1024 = 4.13588e-05 + 0.999923 * (_ctx_1024t + 0.3 * jax.random.normal(jax.random.fold_in(_rk, 611), (2, 512, 128), jnp.float32))
        return (x, ctx_1024)
    x, ctx_1024 = _rec_inputs()

    def _L0_xattn_setup():
        import jax, jax.numpy as jnp
        import numpy as np
        D, H, E, K, DFF = (128, 16, 8, 2, 512)
        B, L, T = (4, 64, 256)
        EPS = 1e-05

        def _xavier(key, shape):
            fan_in, fan_out = (shape[-1], shape[-2])
            a = jnp.sqrt(6.0 / (fan_in + fan_out))
            return jax.random.uniform(key, shape, jnp.float32, -a, a)

        def _ln(x, g, b):
            m = x.mean(-1, keepdims=True)
            v = ((x - m) ** 2).mean(-1, keepdims=True)
            return (x - m) / jnp.sqrt(v + EPS) * g + b

        def _mha(q_in, kv_in, in_w, in_b, out_w, out_b):
            wq, wk, wv = jnp.split(in_w, 3, axis=0)
            bq, bk, bv = jnp.split(in_b, 3, axis=0)
            dh = D // H

            def heads(x, w, b):
                y = x @ w.T + b
                return y.reshape(x.shape[0], x.shape[1], H, dh).transpose(0, 2, 1, 3)
            q = heads(q_in, wq, bq)
            k = heads(kv_in, wk, bk)
            v = heads(kv_in, wv, bv)
            scores = jnp.einsum('bhqd,bhkd->bhqk', q, k) / jnp.sqrt(jnp.float32(dh))
            attn = jax.nn.softmax(scores, axis=-1)
            out = jnp.einsum('bhqk,bhkd->bhqd', attn, v)
            out = out.transpose(0, 2, 1, 3).reshape(q_in.shape[0], q_in.shape[1], D)
            return out @ out_w.T + out_b

        def _fuse_moe(x, ln_g, ln_b, rw, rb, fc1_w, fc1_b, fc2_w, fc2_b):
            h = _ln(x, ln_g, ln_b)
            logits = h @ rw.T + rb
            vals, idx = jax.lax.top_k(logits, K)
            gates = jax.nn.softmax(vals, axis=-1)
            N = x.shape[0] * x.shape[1]
            hf = h.reshape(N, D)
            h1 = jax.nn.gelu(jnp.einsum('nd,efd->enf', hf, fc1_w) + fc1_b[:, None, :], approximate=False)
            eo = jnp.einsum('enf,edf->end', h1, fc2_w) + fc2_b[:, None, :]
            idx_f = idx.reshape(N, K)
            gates_f = gates.reshape(N, K)
            gathered = eo[idx_f, jnp.arange(N)[:, None], :]
            mixed = (gathered * gates_f[..., None]).sum(axis=1).reshape(x.shape)
            return x + mixed
        key = jax.random.key(seed)
        ks = jax.random.split(key, 16)
        inp = {'latents': jax.random.normal(ks[0], (B, L, D), jnp.float32), 'tokens': jax.random.normal(ks[1], (B, T, D), jnp.float32), 'sa_ln_g': jnp.ones((D,)), 'sa_ln_b': jnp.zeros((D,)), 'sa_in_w': _xavier(ks[2], (3 * D, D)), 'sa_in_b': jnp.zeros((3 * D,)), 'sa_out_w': _xavier(ks[3], (D, D)), 'sa_out_b': jnp.zeros((D,)), 'ca_q_ln_g': jnp.ones((D,)), 'ca_q_ln_b': jnp.zeros((D,)), 'ca_kv_ln_g': jnp.ones((D,)), 'ca_kv_ln_b': jnp.zeros((D,)), 'ca_in_w': _xavier(ks[4], (3 * D, D)), 'ca_in_b': jnp.zeros((3 * D,)), 'ca_out_w': _xavier(ks[5], (D, D)), 'ca_out_b': jnp.zeros((D,)), 'moe_ln_g': jnp.ones((D,)), 'moe_ln_b': jnp.zeros((D,)), 'router_w': _xavier(ks[6], (E, D)), 'router_b': jnp.zeros((E,)), 'e_fc1_w': jax.vmap(lambda k: _xavier(k, (DFF, D)))(jax.random.split(ks[7], E)), 'e_fc1_b': jnp.zeros((E, DFF)), 'e_fc2_w': jax.vmap(lambda k: _xavier(k, (D, DFF)))(jax.random.split(ks[8], E)), 'e_fc2_b': jnp.zeros((E, D))}
        return inp
    _L0_xattn_all = _L0_xattn_setup()
    _L0_xattn_in = {k: v for k, v in _L0_xattn_all.items() if k in ('sa_ln_g', 'sa_ln_b', 'sa_in_w', 'sa_in_b', 'sa_out_w', 'sa_out_b', 'ca_q_ln_g', 'ca_q_ln_b', 'ca_kv_ln_g', 'ca_kv_ln_b', 'ca_in_w', 'ca_in_b', 'ca_out_w', 'ca_out_b', 'moe_ln_g', 'moe_ln_b', 'router_w', 'router_b', 'e_fc1_w', 'e_fc1_b', 'e_fc2_w', 'e_fc2_b')}
    del _L0_xattn_all
    return {'x': x, 'ctx_1024': ctx_1024, 'L0_xattn_sa_ln_g': _L0_xattn_in['sa_ln_g'], 'L0_xattn_sa_ln_b': _L0_xattn_in['sa_ln_b'], 'L0_xattn_sa_in_w': _L0_xattn_in['sa_in_w'], 'L0_xattn_sa_in_b': _L0_xattn_in['sa_in_b'], 'L0_xattn_sa_out_w': _L0_xattn_in['sa_out_w'], 'L0_xattn_sa_out_b': _L0_xattn_in['sa_out_b'], 'L0_xattn_ca_q_ln_g': _L0_xattn_in['ca_q_ln_g'], 'L0_xattn_ca_q_ln_b': _L0_xattn_in['ca_q_ln_b'], 'L0_xattn_ca_kv_ln_g': _L0_xattn_in['ca_kv_ln_g'], 'L0_xattn_ca_kv_ln_b': _L0_xattn_in['ca_kv_ln_b'], 'L0_xattn_ca_in_w': _L0_xattn_in['ca_in_w'], 'L0_xattn_ca_in_b': _L0_xattn_in['ca_in_b'], 'L0_xattn_ca_out_w': _L0_xattn_in['ca_out_w'], 'L0_xattn_ca_out_b': _L0_xattn_in['ca_out_b'], 'L0_xattn_moe_ln_g': _L0_xattn_in['moe_ln_g'], 'L0_xattn_moe_ln_b': _L0_xattn_in['moe_ln_b'], 'L0_xattn_router_w': _L0_xattn_in['router_w'], 'L0_xattn_router_b': _L0_xattn_in['router_b'], 'L0_xattn_e_fc1_w': _L0_xattn_in['e_fc1_w'], 'L0_xattn_e_fc1_b': _L0_xattn_in['e_fc1_b'], 'L0_xattn_e_fc2_w': _L0_xattn_in['e_fc2_w'], 'L0_xattn_e_fc2_b': _L0_xattn_in['e_fc2_b']}

def reference(x, ctx_1024, L0_xattn_sa_ln_g, L0_xattn_sa_ln_b, L0_xattn_sa_in_w, L0_xattn_sa_in_b, L0_xattn_sa_out_w, L0_xattn_sa_out_b, L0_xattn_ca_q_ln_g, L0_xattn_ca_q_ln_b, L0_xattn_ca_kv_ln_g, L0_xattn_ca_kv_ln_b, L0_xattn_ca_in_w, L0_xattn_ca_in_b, L0_xattn_ca_out_w, L0_xattn_ca_out_b, L0_xattn_moe_ln_g, L0_xattn_moe_ln_b, L0_xattn_router_w, L0_xattn_router_b, L0_xattn_e_fc1_w, L0_xattn_e_fc1_b, L0_xattn_e_fc2_w, L0_xattn_e_fc2_b):
    import jax
    import jax.numpy as jnp

    def _L0_xattn_ref(latents, tokens, sa_ln_g, sa_ln_b, sa_in_w, sa_in_b, sa_out_w, sa_out_b, ca_q_ln_g, ca_q_ln_b, ca_kv_ln_g, ca_kv_ln_b, ca_in_w, ca_in_b, ca_out_w, ca_out_b, moe_ln_g, moe_ln_b, router_w, router_b, e_fc1_w, e_fc1_b, e_fc2_w, e_fc2_b):
        import jax, jax.numpy as jnp
        import numpy as np
        D, H, E, K, DFF = (128, 16, 8, 2, 512)
        B, L, T = (4, 64, 256)
        EPS = 1e-05

        def _xavier(key, shape):
            fan_in, fan_out = (shape[-1], shape[-2])
            a = jnp.sqrt(6.0 / (fan_in + fan_out))
            return jax.random.uniform(key, shape, jnp.float32, -a, a)

        def _ln(x, g, b):
            m = x.mean(-1, keepdims=True)
            v = ((x - m) ** 2).mean(-1, keepdims=True)
            return (x - m) / jnp.sqrt(v + EPS) * g + b

        def _mha(q_in, kv_in, in_w, in_b, out_w, out_b):
            wq, wk, wv = jnp.split(in_w, 3, axis=0)
            bq, bk, bv = jnp.split(in_b, 3, axis=0)
            dh = D // H

            def heads(x, w, b):
                y = x @ w.T + b
                return y.reshape(x.shape[0], x.shape[1], H, dh).transpose(0, 2, 1, 3)
            q = heads(q_in, wq, bq)
            k = heads(kv_in, wk, bk)
            v = heads(kv_in, wv, bv)
            scores = jnp.einsum('bhqd,bhkd->bhqk', q, k) / jnp.sqrt(jnp.float32(dh))
            attn = jax.nn.softmax(scores, axis=-1)
            out = jnp.einsum('bhqk,bhkd->bhqd', attn, v)
            out = out.transpose(0, 2, 1, 3).reshape(q_in.shape[0], q_in.shape[1], D)
            return out @ out_w.T + out_b

        def _fuse_moe(x, ln_g, ln_b, rw, rb, fc1_w, fc1_b, fc2_w, fc2_b):
            h = _ln(x, ln_g, ln_b)
            logits = h @ rw.T + rb
            vals, idx = jax.lax.top_k(logits, K)
            gates = jax.nn.softmax(vals, axis=-1)
            N = x.shape[0] * x.shape[1]
            hf = h.reshape(N, D)
            h1 = jax.nn.gelu(jnp.einsum('nd,efd->enf', hf, fc1_w) + fc1_b[:, None, :], approximate=False)
            eo = jnp.einsum('enf,edf->end', h1, fc2_w) + fc2_b[:, None, :]
            idx_f = idx.reshape(N, K)
            gates_f = gates.reshape(N, K)
            gathered = eo[idx_f, jnp.arange(N)[:, None], :]
            mixed = (gathered * gates_f[..., None]).sum(axis=1).reshape(x.shape)
            return x + mixed
        q = _ln(latents, sa_ln_g, sa_ln_b)
        x = latents + _mha(q, q, sa_in_w, sa_in_b, sa_out_w, sa_out_b)
        qc = _ln(x, ca_q_ln_g, ca_q_ln_b)
        kv = _ln(tokens, ca_kv_ln_g, ca_kv_ln_b)
        x = x + _mha(qc, kv, ca_in_w, ca_in_b, ca_out_w, ca_out_b)
        return _fuse_moe(x, moe_ln_g, moe_ln_b, router_w, router_b, e_fc1_w, e_fc1_b, e_fc2_w, e_fc2_b)
    x = _L0_xattn_ref(x, ctx_1024, L0_xattn_sa_ln_g, L0_xattn_sa_ln_b, L0_xattn_sa_in_w, L0_xattn_sa_in_b, L0_xattn_sa_out_w, L0_xattn_sa_out_b, L0_xattn_ca_q_ln_g, L0_xattn_ca_q_ln_b, L0_xattn_ca_kv_ln_g, L0_xattn_ca_kv_ln_b, L0_xattn_ca_in_w, L0_xattn_ca_in_b, L0_xattn_ca_out_w, L0_xattn_ca_out_b, L0_xattn_moe_ln_g, L0_xattn_moe_ln_b, L0_xattn_router_w, L0_xattn_router_b, L0_xattn_e_fc1_w, L0_xattn_e_fc1_b, L0_xattn_e_fc2_w, L0_xattn_e_fc2_b)
    return x

_drawn_inputs = setup_inputs


def setup_inputs(seed=0):
    import zlib

    import numpy as np

    out = dict(_drawn_inputs(seed))
    spreads = {'L0_xattn_sa_ln_g': (1.0, 0.2),
     'L0_xattn_sa_ln_b': (0.0, 0.1),
     'L0_xattn_sa_in_b': (0.0, 0.1),
     'L0_xattn_sa_out_b': (0.0, 0.1),
     'L0_xattn_ca_q_ln_g': (1.0, 0.2),
     'L0_xattn_ca_q_ln_b': (0.0, 0.314),
     'L0_xattn_ca_kv_ln_g': (1.0, 0.2),
     'L0_xattn_ca_kv_ln_b': (0.0, 0.1),
     'L0_xattn_ca_in_b': (0.0, 0.1),
     'L0_xattn_ca_out_b': (0.0, 0.1),
     'L0_xattn_moe_ln_g': (1.0, 0.2),
     'L0_xattn_moe_ln_b': (0.0, 0.1),
     'L0_xattn_router_b': (0.0, 0.1),
     'L0_xattn_e_fc1_b': (0.0, 0.1),
     'L0_xattn_e_fc2_b': (0.0, 0.1)}
    factors = {}
    for name, (base, spread) in spreads.items():
        noise = np.random.default_rng([zlib.crc32(name.encode()), seed]).standard_normal(out[name].shape)
        drawn = base * np.exp(spread * noise) if base else spread * noise
        out[name] = jnp.asarray(drawn.astype(out[name].dtype))
    for name, factor in factors.items():
        out[name] = (out[name] * factor).astype(out[name].dtype)
    return out
```

```python
from contextlib import ExitStack

import concourse.bass as bass
from concourse import mybir

F32 = mybir.dt.float32
BF16 = mybir.dt.bfloat16
ALU = mybir.AluOpType
ACT = mybir.ActivationFunctionType
AXX = mybir.AxisListType.X

D, H, E, DFF, B = 128, 16, 8, 512, 2
DH = D // H
L, S = 256, 512
EPS = 1e-5
SCALE = DH ** -0.5
NC1 = DFF // D
QT = L // 128
HALF = 8
NP_TILES = 16
S1_BANKS, S2_BANKS = 2, 3
MAXROW = 48

(SA_G, SA_B, CQ_G, CQ_B, CKV_G, CKV_B, MOE_G, MOE_B, SA_BQ, SA_BK, CA_BQ, CA_BK, FC1_B) = range(13)
NCOLS = FC1_B + E * NC1
SQ, SK, SV, SO, CQ, CK, CV, CO = range(8)
SA_BV, SA_BO, CA_BV, CA_BO = range(4)

GAP = 8
LAG = 4


def nkc(i):
    return 2 if i < 4 else 4


def pass1_start(i):
    return 8 * i + (GAP if i >= 4 else 0)


def pass2_start(i):
    return pass1_start(i) + 8 + LAG


N_STEPS = pass2_start(7) + 8 + 2
BASE = [0, 8, 16, 24, 32, 48, 64, 80, 96]

AFTER = {t: [] for t in range(-1, N_STEPS + 16)}
AFTER[-1] = [("xT", 0), ("qk", 0), ("xT", 1), ("qk", 1), ("v", 0), ("v", 1)]
for _i in range(8):
    AFTER[pass1_start(_i) + 8].append(("m", _i))
for _t, _x in ((0, ("cn", 0)), (2, ("cT", 0)), (3, ("ck", 0)), (5, ("cv", 0)),
               (35, ("cn", 1)), (37, ("cT", 1)), (38, ("ck", 1)), (39, ("cv", 1))):
    AFTER[_t].append(_x)
for _b in range(B):
    _t = pass2_start(2 * _b + 1) + 4 + 3 + 2
    AFTER[_t + 1] += [("oT", _b, 0), ("oT", _b, 1)]
    AFTER[_t + 2].append(("aT", _b))
    AFTER[_t + 3].append(("op", _b))
    AFTER[_t + 4].append(("yT", _b))
    AFTER[_t + 5].append(("cq", _b))
_t = pass2_start(5) + 4 + 3 + 2
for _k, _x in ((1, ("oT", 2, 0)), (1, ("oT", 2, 1)), (2, ("aT", 2)), (3, ("op", 2)),
               (5, ("wT", 0)), (6, ("rt", 0)), (8, ("gT", 0)), (9, ("b2", 0))):
    AFTER[_t + _k].append(_x)
for _k, _x in ((0, ("oT", 3, 0)), (0, ("oT", 3, 1)), (1, ("aT", 3)), (2, ("op", 3)),
               (3, ("wT", 1)), (4, ("rt", 1)), (5, ("gT", 1)), (6, ("b2", 1))):
    AFTER[N_STEPS + _k].append(_x)

MISC = {x: n for n, x in enumerate(
    x for t in range(-1, N_STEPS + 16) for x in AFTER[t] if x[0] != "cn")}
SPLITS = [x for x in MISC if x[0] in ("qk", "ck", "cq")]
NORMS = [("x", 0), ("x", 1)] + [
    {"cn": ("c", x[1]), "op": ("y" if x[1] < 2 else "w", x[1] % 2)}[x[0]]
    for t in range(-1, N_STEPS + 16) for x in AFTER[t] if x[0] in ("cn", "op")]


def pass1_at(t):
    return next(((i, t - pass1_start(i)) for i in range(8) if 0 <= t - pass1_start(i) < 8), None)


def pass2_at(t):
    return next(((i, t - pass2_start(i)) for i in range(8) if 0 <= t - pass2_start(i) < 8), None)


def av_at(t):
    return next(((i, g) for i in range(8) for g in range(2) if t == pass2_start(i) + 4 * g + 5), None)


def xattn_moe(nc, x, ctx_in, attn_w, cols, rows, rb, w1, w2, rw, b2, ident, tri, out):
    with ExitStack() as stack:
        def sb(name, shape, dt=F32):
            return stack.enter_context(nc.sbuf_tensor(name, shape, dt))

        def ps(name, shape, dt=F32):
            return stack.enter_context(nc.psum_tensor(name, shape, dt))

        def sem(name):
            return stack.enter_context(nc.semaphore(name))

        x_sb = sb("x_sb", [128, B * QT, D])
        c_sb = sb("c_sb", [128, B * 4, D])
        aw = sb("aw", [128, 8, D])
        col = sb("col", [128, NCOLS])
        row = sb("row", [128, 4, D])
        rb_bc = sb("rb_bc", [128, E])
        w1_sb = sb("w1_sb", [128, E, NC1, D])
        w2_sb = sb("w2_sb", [128, E, NC1, D])
        rw_sb = sb("rw_sb", [128, E])
        b2_sb = sb("b2_sb", [E, D])
        idf = sb("idf", [128, 128])
        idb = sb("idb", [128, 128], BF16)
        tri_sb = sb("tri_sb", [128, E, E])
        stats = sb("stats", [128, 4, 6])
        mv = sb("mv", [128, len(NORMS), 4, 2])
        veps = sb("veps", [128, len(NORMS), 4])
        rstd = sb("rstd", [128, len(NORMS), 4])
        mhalf = sb("mhalf", [128, 4])
        z_lat = sb("z_lat", [128, B * QT, D])
        zx = zy = z_lat
        zc = c_sb
        xT = sb("xT", [128, B, L])
        cT = sb("cT", [128, B, S])
        yT = wT = xT
        v_self = sb("v_self", [128, B, 2, H, DH + 1])
        v_cross = sb("v_cross", [128, B, 4, H, DH + 1])
        part_qk = sb("part_qk", [128, B, 2, 3, L], BF16)
        part_ck = sb("part_ck", [128, B, 3, S], BF16)
        part_cq = part_qk[:, :, 0]
        rest = sb("rest", [128, 512])
        q_op = sb("q_op", [128, 4, H, L], BF16)
        k_self = sb("k_self", [128, B, H, L], BF16)
        k_cross = sb("k_cross", [128, B, H, S], BF16)
        negmax = sb("negmax", [128, 2, QT, HALF])
        negmax_parts = sb("negmax_parts", [128, 2, QT, 2, HALF], BF16)
        negmaxT = sb("negmaxT", [2 * HALF, 2, L], BF16)
        probs = sb("probs", [128, NP_TILES, 512])
        av_sb = sb("av_sb", [128, 2, 4, L])
        rsum = sb("rsum", [128, QT, H])
        attn = sb("attn", [128, QT, D])
        attnT = sb("attnT", [128, L])
        res = sb("res", [128, B * QT, D])
        x1 = sb("x1", [128, B * QT, D])
        res2 = res
        x2 = x1
        lg = sb("lg", [128, QT, E])
        top = sb("top", [128, QT])
        above = sb("above", [128, QT, E, E])
        ties = sb("ties", [128, QT, E, E])
        rank = sb("rank", [128, QT, E])
        shifted = sb("shifted", [128, QT, E])
        ex = sb("ex", [128, QT, E])
        den = sb("den", [128, QT])
        gates = sb("gates", [128, B, QT, E])
        gatesT = sb("gatesT", [E, B, L])
        acc = x1

        s1 = ps("s1", [128, S1_BANKS, 512])
        s2 = ps("s2", [128, S2_BANKS, 512])
        avp = ps("avp", [128, 512])
        misc = ps("misc", [128, 2, 512])
        fc1_ring = [s1[:, 0, :], s1[:, 1, :], s2[:, 0, :], s2[:, 1, :]]
        fc2_ring = [avp[:, :], s2[:, 2, :]]

        scr_qk = [nc.dram_tensor(f"scr_qk{b}", [2, 3, D, L], BF16, kind="Internal").ap() for b in range(B)]
        scr_ck = [nc.dram_tensor(f"scr_ck{b}", [3, D, S], BF16, kind="Internal").ap() for b in range(B)]
        scr_cq = [nc.dram_tensor(f"scr_cq{b}", [3, D, L], BF16, kind="Internal").ap() for b in range(B)]

        ld_x = [sem(f"ld_x{b}") for b in range(B)]
        ld_c = [sem(f"ld_c{b}") for b in range(B)]
        ld_aw, ld_aw2, ld_col, ld_row, ld_rb = sem("ld_aw"), sem("ld_aw2"), sem("ld_col"), sem("ld_row"), sem("ld_rb")
        ld_w1, ld_w2, ld_rw, ld_b2 = sem("ld_w1"), sem("ld_w2"), sem("ld_rw"), sem("ld_b2")
        ld_id, ld_tri = sem("ld_id"), sem("ld_tri")
        idb_ready, mhalf_ready, v_ones, av_zero = sem("idb_ready"), sem("mhalf_ready"), sem("v_ones"), sem("av_zero")
        q_wiped = [sem(f"q_wiped{k}") for k in range(4)]
        k_wiped = [sem(f"k_wiped{k}") for k in range(4)]
        var_ready, rstd_ready = sem("var_ready"), sem("rstd_ready")
        z_ready = {n: sem(f"z{n[0]}{n[1]}") for n in NORMS}
        misc_full = [sem(f"misc_full{k}") for k in range(2)]
        misc_read = [sem(f"misc_read{k}") for k in range(2)]
        xT_ready, cT_ready, yT_ready, wT_ready = sem("xT_ready"), sem("cT_ready"), sem("yT_ready"), sem("wT_ready")
        hi_ready, parts_ready = sem("hi_ready"), sem("parts_ready")
        scr_written = [sem(f"scr_written{k}") for k in range(len(SPLITS))]
        q_ready = [sem(f"q_ready{k}") for k in range(4)]
        k_ready = [sem(f"k_ready{k}") for k in range(4)]
        s1_full, s1_read = sem("s1_full"), sem("s1_read")
        negmax_ready = sem("negmax_ready")
        negmaxT_ready = sem("negmaxT_ready")
        max_rows = [sem(f"max_rows{i}") for i in range(8)]
        s2_full, probs_ready = sem("s2_full"), sem("probs_ready")
        av_full, av_read = sem("av_full"), sem("av_read")
        res_ready, res2_ready = sem("res_ready"), sem("res2_ready")
        shifted_ready, ex_ready, gates_ready, gatesT_ready = (
            sem("shifted_ready"), sem("ex_ready"), sem("gates_ready"), sem("gatesT_ready"))
        fc1_full, gelu_ready, fc2_full, acc_step = sem("fc1_full"), sem("gelu_ready"), sem("fc2_full"), sem("acc_step")
        stored = sem("stored")
        dve_own, act_own = sem("dve_own"), sem("act_own")

        def bank(item):
            return MISC[item] % 2

        def wait_full(eng, item):
            eng.wait_ge(misc_full[bank(item)], MISC[item] // 2 + 1)

        def wait_free(eng, item):
            if MISC[item] // 2 > 0:
                eng.wait_ge(misc_read[bank(item)], MISC[item] // 2)

        def wait_read(eng, item):
            eng.wait_ge(misc_read[bank(item)], MISC[item] // 2 + 1)

        block = stack.enter_context(nc.Block())

        @block.sync
        def _(sp):
            tok = x.rearrange("(t p) d -> p t d", p=128)
            ctok = ctx_in.rearrange("(t p) d -> p t d", p=128)
            for b in range(B):
                sp.dma_start(x_sb[:, QT * b:QT * (b + 1), :], tok[:, QT * b:QT * (b + 1), :]).then_inc(ld_x[b], 16)
                if b == 0:
                    sp.dma_start(idf[:, :], ident).then_inc(ld_id, 16)
                    sp.dma_start(col[:, :], cols).then_inc(ld_col, 16)
                    sp.dma_start(aw[:, 0:4, :], attn_w[:, 0:4, :]).then_inc(ld_aw, 16)
            sp.dma_start(row[:, :, :], rows.unsqueeze(0).broadcast_to([128, 4, D])).then_inc(ld_row, 16)
            for b in range(B):
                sp.dma_start(c_sb[:, 4 * b:4 * b + 4, :], ctok[:, 4 * b:4 * b + 4, :]).then_inc(ld_c[b], 16)
            sp.dma_start(aw[:, 4:8, :], attn_w[:, 4:8, :]).then_inc(ld_aw2, 16)

            for j, item in enumerate(SPLITS):
                kind, b = item
                sp.wait_ge(parts_ready, j + 1)
                if kind == "qk":
                    sp.dma_start(scr_qk[b].rearrange("a t p c -> p (a t) c"),
                                 part_qk[:, b].rearrange("p a t c -> p (a t) c")).then_inc(scr_written[j], 16)
                elif kind == "ck":
                    sp.dma_start(scr_ck[b].rearrange("t p c -> p t c"), part_ck[:, b]).then_inc(scr_written[j], 16)
                else:
                    sp.dma_start(scr_cq[b].rearrange("t p c -> p t c"), part_cq[:, b]).then_inc(scr_written[j], 16)
                sp.wait_ge(scr_written[j], 16)
                blk = b if kind == "qk" else 2 + b
                if kind != "ck":
                    src = (scr_qk[b][0] if kind == "qk" else scr_cq[b]).rearrange("t (d h) c -> t d h c", d=DH)
                    sp.wait_ge(q_wiped[blk], 1)
                    for slot, part in enumerate((0, 0, 0, 1, 1, 2)):
                        sp.dma_start(q_op[DH * slot:DH * (slot + 1), blk], src[part]).then_inc(q_ready[blk], 16)
                if kind != "cq":
                    src = (scr_qk[b][1] if kind == "qk" else scr_ck[b]).rearrange("t (d h) c -> (t d) h c", d=DH)
                    dst = k_self[:, b] if kind == "qk" else k_cross[:, b]
                    sp.wait_ge(k_wiped[blk], 1)
                    for slot, parts in ((0, 3), (3, 2), (5, 1)):
                        sp.dma_start(dst[DH * slot:DH * (slot + parts)], src[0:DH * parts]).then_inc(k_ready[blk], 16)
                if j == 1:
                    sp.dma_start(rb_bc[:, :], rb.unsqueeze(0).broadcast_to([128, E])).then_inc(ld_rb, 16)
                    sp.dma_start(tri_sb[:, :, :], tri).then_inc(ld_tri, 16)
                    sp.dma_start(rw_sb[:, :], rw).then_inc(ld_rw, 16)
                    sp.dma_start(b2_sb[:, :], b2).then_inc(ld_b2, 16)
                    sp.dma_start(w1_sb[:, :, :, :], w1).then_inc(ld_w1, 16)
                    sp.dma_start(w2_sb[:, :, :, :], w2).then_inc(ld_w2, 16)
            out_t = out.rearrange("(t p) d -> p t d", p=128)
            for b in range(B):
                sp.wait_ge(acc_step, E * (b + 1))
                sp.dma_start(out_t[:, QT * b:QT * (b + 1), :], acc[:, QT * b:QT * (b + 1), :]).then_inc(stored, 16)
            sp.wait_ge(stored, 16 * B)

        @block.gpsimd
        def _(pool):
            def power(n):
                w = 4 if NORMS[n][0] == "c" else QT
                pool.wait_ge(var_ready, n + 1)
                nc.gpsimd.tensor_tensor(rstd[:, n, 0:w], veps[:, n, 0:w], mhalf[:, 0:w], ALU.pow).then_inc(rstd_ready, 1)

            def wipe(blk, q=True, k=True):
                if q:
                    nc.gpsimd.memset(q_op[:, blk], 0.0).then_inc(q_wiped[blk], 1)
                if k:
                    nc.gpsimd.memset(k_self[:, blk] if blk < 2 else k_cross[:, blk - 2], 1.0).then_inc(k_wiped[blk], 1)

            nc.gpsimd.memset(mhalf[:, :], -0.5).then_inc(mhalf_ready, 1)
            wipe(0, q=False)
            pool.wait_ge(mhalf_ready, 1)
            power(0)
            power(1)
            nc.gpsimd.memset(v_self[:], 1.0)
            nc.gpsimd.memset(v_cross[:], 1.0).then_inc(v_ones, 1)
            wipe(1)
            pool.wait_ge(ld_row, 16)
            for b in range(B):
                pool.wait_ge(ld_x[b], 16)
            for t in range(B * QT):
                last = nc.gpsimd.tensor_tensor(res[:, t, :], x_sb[:, t, :], row[:, SA_BO, :], ALU.add)
            last.then_inc(res_ready, 1)
            for n in range(2, len(NORMS)):
                name, b = NORMS[n]
                power(n)
                if name == "c":
                    wipe(2 + b)
                elif name == "y":
                    wait_read(pool, ("op", b))
                    for t in range(QT * b, QT * (b + 1)):
                        last = nc.gpsimd.tensor_tensor(res2[:, t, :], x1[:, t, :], row[:, CA_BO, :], ALU.add)
                    last.then_inc(res2_ready, 1)

        @block.scalar
        def _(act):
            def identity(dst, src, bias, scale=1.0):
                return nc.scalar.activation(dst, src, ACT.Identity, bias=bias, scale=scale)

            def c(j):
                return col[:, j:j + 1]

            def extra(item):
                kind, idx = item[0], item[1]
                if kind in ("cn", "rt", "v", "cv", "op", "oT", "b2"):
                    if kind == "rt":
                        act.wait_ge(shifted_ready, idx + 1)
                        nc.scalar.activation(ex[:, :, :], shifted[:, :, :], ACT.Exp).then_inc(ex_ready, 1)
                    return
                wait_full(act, item)
                m = misc[:, bank(item), :]
                free = misc_read[bank(item)]
                if kind == "xT":
                    identity(xT[:, idx, :], m[:, 0:L], c(SA_B), c(SA_G)).then_inc(free, 1)
                elif kind == "cT":
                    identity(cT[:, idx, :], m[:, 0:S], c(CKV_B), c(CKV_G)).then_inc(free, 1)
                elif kind == "yT":
                    identity(yT[:, idx, :], m[:, 0:L], c(CQ_B), c(CQ_G)).then_inc(free, 1)
                elif kind == "wT":
                    identity(wT[:, idx, :], m[:, 0:L], c(MOE_B), c(MOE_G)).then_inc(free, 1)
                elif kind == "qk":
                    identity(part_qk[:, idx, 0, 0, :], m[:, 0:L], c(SA_BQ))
                    identity(part_qk[:, idx, 1, 0, :], m[:, L:2 * L], c(SA_BK)).then_inc(hi_ready, 1)
                elif kind == "ck":
                    identity(part_ck[:, idx, 0, :], m[:, 0:S], c(CA_BK)).then_inc(hi_ready, 1)
                elif kind == "cq":
                    identity(part_cq[:, idx, 0, :], m[:, 0:L], c(CA_BQ)).then_inc(hi_ready, 1)
                elif kind == "aT":
                    nc.scalar.copy(attnT[:, :], m[:, 0:L]).then_inc(free, 1)
                elif kind == "gT":
                    nc.scalar.copy(gatesT[:, idx, :], m[0:E, 0:L]).then_inc(free, 1)
                elif kind == "m":
                    i = idx
                    if i >= 2:
                        act.wait_ge(max_rows[i - 2], 32)
                    nc.scalar.copy(negmaxT[:, i % 2, :], m.bitcast(BF16)[0:2 * HALF, 0:L]).then_inc(free, 1)
                    wait_read(act, item)
                    for part in range(2):
                        act.dma_start(q_op[MAXROW + part:MAXROW + part + 1, i // 2, HALF * (i % 2):HALF * (i % 2 + 1), :],
                                      negmaxT[HALF * part:HALF * (part + 1), i % 2, :]).then_inc(max_rows[i], 16)

            act.wait_ge(ld_col, 16)
            for item in AFTER[-1]:
                extra(item)
            for t in range(N_STEPS):
                if pass2_at(t):
                    i, s = pass2_at(t)
                    for k in range(nkc(i) // 2):
                        n = BASE[i] + s * (nkc(i) // 2) + k
                        act.wait_ge(s2_full, n + 1)
                        if n >= NP_TILES:
                            old = n - NP_TILES
                            oi = max(q for q in range(8) if BASE[q] <= old)
                            act.wait_ge(av_full, 2 * oi + (old - BASE[oi]) // (4 * nkc(oi) // 2) + 1)
                        nc.scalar.activation(probs[:, n % NP_TILES, :], s2[:, n % S2_BANKS, :], ACT.Exp,
                                             scale=SCALE).then_inc(probs_ready, 1)
                if av_at(t):
                    i, g = av_at(t)
                    a = 2 * i + g
                    act.wait_ge(av_full, a + 1)
                    if a >= 8:
                        wait_full(act, ("oT", a // 4 - 2, 1))
                    nc.scalar.copy(av_sb[:, (a // 4) % 2, a % 4, :], avp[:, 0:L]).then_inc(av_read, 1)
                for item in AFTER[t]:
                    extra(item)
            for n in range(B * E):
                b, e = divmod(n, E)
                for cp in range(2):
                    act.wait_ge(fc1_full, 2 * n + cp + 1)
                    if n >= 3 and cp == 0:
                        act.wait_ge(fc2_full, n - 2)
                    for q in range(2):
                        k = 2 * cp + q
                        last = nc.scalar.activation(
                            probs[:, 2 * (n % 3) + cp, L * q:L * (q + 1)], fc1_ring[(2 * n + cp) % 4][:, L * q:L * (q + 1)],
                            ACT.Gelu, bias=col[:, FC1_B + e * NC1 + k:FC1_B + e * NC1 + k + 1])
                    last.then_inc(gelu_ready, 1)
                for item in AFTER[N_STEPS + n]:
                    extra(item)

        @block.vector
        def _(dve):
            own = [0]

            def link(ins):
                own[0] += 1
                ins.then_inc(dve_own, 1)
                dve.wait_ge(dve_own, own[0])

            def norm(name, src, z, w):
                n = NORMS.index(name)
                for t in range(w):
                    last = nc.vector.bn_stats(stats[:, t, :], src[:, t, :])
                link(last)
                for t in range(w):
                    last = nc.vector.bn_aggr(mv[:, n, t, :], stats[:, t, :])
                link(last)
                nc.vector.tensor_scalar_add(veps[:, n, 0:w], mv[:, n, 0:w, 1], EPS).then_inc(var_ready, 1)
                dve.wait_ge(rstd_ready, n + 1)
                for t in range(w):
                    last = nc.vector.tensor_scalar(z[:, t, :], src[:, t, :], mv[:, n, t, 0:1], rstd[:, n, t:t + 1],
                                                   ALU.subtract, ALU.mult)
                last.then_inc(z_ready[name], 1)

            def negmax_split(i):
                dve.wait_ge(s1_read, BASE[i + 1])
                if i >= 2:
                    dve.wait_ge(misc_full[bank(("m", i - 2))], MISC[("m", i - 2)] // 2 + 1)
                link(nc.vector.tensor_copy(negmax_parts[:, i % 2, :, 0, :], negmax[:, i % 2]))
                nc.vector.tensor_tensor(negmax_parts[:, i % 2, :, 1, :], negmax[:, i % 2],
                                        negmax_parts[:, i % 2, :, 0, :], ALU.subtract).then_inc(negmax_ready, 1)

            def split(item, dsts, bias_cols):
                j = SPLITS.index(item)
                m = misc[:, bank(item), :]
                wait_full(dve, item)
                dve.wait_ge(hi_ready, j + 1)
                at = 0
                for dst, bias in zip(dsts, bias_cols):
                    w = dst.shape[-1]
                    last = nc.vector.scalar_tensor_tensor(rest[:, at:at + w], m[:, at:at + w], col[:, bias:bias + 1],
                                                          dst[:, 0, :], ALU.add, ALU.subtract)
                    at += w
                last.then_inc(misc_read[bank(item)], 1)
                wait_read(dve, item)
                at = 0
                for dst in dsts:
                    w = dst.shape[-1]
                    last = nc.vector.tensor_copy(dst[:, 1, :], rest[:, at:at + w])
                    at += w
                link(last)
                at = 0
                for dst in dsts:
                    w = dst.shape[-1]
                    last = nc.vector.tensor_tensor(dst[:, 2, :], rest[:, at:at + w], dst[:, 1, :], ALU.subtract)
                    at += w
                last.then_inc(parts_ready, 1)
                dve.wait_ge(parts_ready, j + 1)

            def values(item, v, bias):
                w = 2 if item[0] == "v" else 4
                wait_full(dve, item)
                for t in range(w):
                    last = nc.vector.tensor_tensor(
                        v[:, t, :, 0:DH], misc[:, bank(item), D * t:D * (t + 1)].rearrange("p (h d) -> p h d", d=DH),
                        row[:, bias, :].rearrange("p (h d) -> p h d", d=DH), ALU.add)
                last.then_inc(misc_read[bank(item)], 1)

            def route(b):
                item = ("rt", b)
                wait_full(dve, item)
                m = misc[:, bank(item), 0:QT * E].rearrange("p (t e) -> p t e", e=E)
                nc.vector.tensor_tensor(lg[:, :, :], m, rb_bc[:, :].unsqueeze(1).broadcast_to([128, QT, E]),
                                        ALU.add).then_inc(misc_read[bank(item)], 1)
                wait_read(dve, item)
                link(nc.vector.tensor_reduce(top[:, :], lg[:, :, :], AXX, ALU.max))
                nc.vector.tensor_tensor(shifted[:, :, :], lg[:, :, :], top[:, :].unsqueeze(2).broadcast_to([128, QT, E]),
                                        ALU.subtract).then_inc(shifted_ready, 1)
                mine = lg[:, :, :].unsqueeze(3).broadcast_to([128, QT, E, E])
                others = lg[:, :, :].unsqueeze(2).broadcast_to([128, QT, E, E])
                link(nc.vector.tensor_tensor(ties[:], others, mine, ALU.is_equal))
                link(nc.vector.tensor_tensor(above[:], others, mine, ALU.is_gt))
                link(nc.vector.tensor_tensor(ties[:], ties[:], tri_sb[:, :, :].unsqueeze(1).broadcast_to([128, QT, E, E]),
                                             ALU.mult))
                link(nc.vector.tensor_tensor(above[:], above[:], ties[:], ALU.add))
                link(nc.vector.tensor_reduce(rank[:, :, :], above[:], AXX, ALU.add))
                dve.wait_ge(ex_ready, b + 1)
                link(nc.vector.scalar_tensor_tensor(rank[:, :, :], rank[:, :, :], 1.5, ex[:, :, :], ALU.is_lt, ALU.mult))
                link(nc.vector.tensor_reduce(den[:, :], rank[:, :, :], AXX, ALU.add))
                link(nc.vector.reciprocal(den[:, :], den[:, :]))
                nc.vector.tensor_tensor(gates[:, b], rank[:, :, :], den[:, :].unsqueeze(2).broadcast_to([128, QT, E]),
                                        ALU.mult).then_inc(gates_ready, 1)
                dve.wait_ge(gates_ready, b + 1)

            def extra(item):
                kind, idx = item[0], item[1]
                if kind == "cn":
                    dve.wait_ge(ld_c[idx], 16)
                    norm(("c", idx), c_sb[:, 4 * idx:4 * idx + 4, :], zc[:, 4 * idx:4 * idx + 4, :], 4)
                elif kind == "qk":
                    split(item, [part_qk[:, idx, 0], part_qk[:, idx, 1]], [SA_BQ, SA_BK])
                elif kind == "ck":
                    split(item, [part_ck[:, idx]], [CA_BK])
                elif kind == "cq":
                    split(item, [part_cq[:, idx]], [CA_BQ])
                elif kind == "v":
                    dve.wait_ge(ld_row, 16)
                    dve.wait_ge(v_ones, 1)
                    values(item, v_self[:, idx], SA_BV)
                elif kind == "cv":
                    values(item, v_cross[:, idx], CA_BV)
                elif kind == "oT":
                    blk, qt = item[1:]
                    wait_full(dve, item)
                    o = misc[:, bank(item), :].rearrange("p (h c) -> p h c", c=32)
                    link(nc.vector.reciprocal(rsum[:, qt, :], o[:, :, DH]))
                    if blk:
                        wait_full(dve, ("aT", blk - 1))
                    nc.vector.tensor_tensor(attn[:, qt, :].rearrange("p (h d) -> p h d", d=DH), o[:, :, 0:DH],
                                            rsum[:, qt, :].unsqueeze(2).broadcast_to([128, H, DH]),
                                            ALU.mult).then_inc(misc_read[bank(item)], 1)
                    wait_read(dve, item)
                elif kind == "op":
                    blk, b = idx, idx % 2
                    wait_full(dve, item)
                    ts = slice(QT * b, QT * (b + 1))
                    m = misc[:, bank(item), 0:L].rearrange("p (t d) -> p t d", d=D)
                    if blk < 2:
                        dve.wait_ge(res_ready, 1)
                        nc.vector.tensor_tensor(x1[:, ts, :], m, res[:, ts, :], ALU.add).then_inc(misc_read[bank(item)], 1)
                        wait_read(dve, item)
                        norm(("y", b), x1[:, ts, :], zy[:, ts, :], QT)
                    else:
                        dve.wait_ge(res2_ready, b + 1)
                        nc.vector.tensor_tensor(x2[:, ts, :], m, res2[:, ts, :], ALU.add).then_inc(misc_read[bank(item)], 1)
                        wait_read(dve, item)
                        norm(("w", b), x2[:, ts, :], zx[:, ts, :], QT)
                elif kind == "rt":
                    route(idx)
                elif kind == "b2":
                    wait_full(dve, item)
                    ts = slice(QT * idx, QT * (idx + 1))
                    nc.vector.tensor_tensor(acc[:, ts, :], misc[:, bank(item), 0:L].rearrange("p (t d) -> p t d", d=D),
                                            x2[:, ts, :], ALU.add).then_inc(misc_read[bank(item)], 1)
                    wait_read(dve, item)

            nc.vector.memset(avp[:, :], 0.0).then_inc(av_zero, 1)
            nc.vector.memset(q_op[:, 0], 0.0).then_inc(q_wiped[0], 1)
            for b in range(B):
                dve.wait_ge(ld_x[b], 16)
                norm(("x", b), x_sb[:, QT * b:QT * (b + 1), :], zx[:, QT * b:QT * (b + 1), :], QT)
            dve.wait_ge(ld_id, 16)
            nc.vector.tensor_copy(idb[:, :], idf[:, :]).then_inc(idb_ready, 1)
            dve.wait_ge(ld_col, 16)
            for item in AFTER[-1]:
                extra(item)
            for t in range(N_STEPS):
                for item in AFTER[t]:
                    if item[0] == "m":
                        negmax_split(item[1])
                if pass1_at(t):
                    i, s = pass1_at(t)
                    for k in range(nkc(i) // 2):
                        n = BASE[i] + s * (nkc(i) // 2) + k
                        dve.wait_ge(s1_full, n + 1)
                        src = s1[:, n % S1_BANKS, :]
                        if i < 4:
                            dst = negmax[:, i % 2, s % 2, s - s % 2:s - s % 2 + 2]
                            src = src.rearrange("p (h k) -> p h k", h=2)
                        else:
                            dst = negmax[:, i % 2, k, s:s + 1]
                        nc.vector.tensor_reduce(dst, src, AXX, ALU.max, negate=True).then_inc(s1_read, 1)
                for item in AFTER[t]:
                    extra(item)
            for n in range(B * E + 1):
                if n >= 1:
                    b, e = divmod(n - 1, E)
                    dve.wait_ge(fc2_full, n)
                    for q in range(QT):
                        last = nc.vector.scalar_tensor_tensor(
                            acc[:, QT * b + q, :], fc2_ring[(n - 1) % 2][:, D * q:D * (q + 1)], gates[:, b, q, e:e + 1],
                            acc[:, QT * b + q, :], ALU.mult, ALU.add)
                    last.then_inc(acc_step, 1)
                    dve.wait_ge(acc_step, n)
                if n < B * E:
                    for item in AFTER[N_STEPS + n]:
                        extra(item)

        @block.tensor
        def _(pe):
            def mm(dst, lhsT, rhs, start=True, stop=True):
                return nc.tensor.matmul(dst, lhsT, rhs, start=start, stop=stop)

            def extra(item):
                kind, idx = item[0], item[1]
                if kind == "cn":
                    return
                m = misc[:, bank(item), :]
                wait_free(pe, item)
                if kind in ("xT", "cT", "yT", "wT"):
                    name = {"xT": "x", "cT": "c", "yT": "y", "wT": "w"}[kind]
                    z = {"xT": zx, "cT": zc, "yT": zy, "wT": zx}[kind]
                    w = 4 if kind == "cT" else QT
                    pe.wait_ge(z_ready[(name, idx)], 1)
                    for t in range(w):
                        last = nc.tensor.transpose(m[:, 128 * t:128 * (t + 1)], z[:, w * idx + t, :], idf[:, :])
                elif kind == "qk":
                    wait_read(pe, ("xT", idx))
                    mm(m[:, 0:L], aw[:, SQ, :], xT[:, idx, :])
                    last = mm(m[:, L:2 * L], aw[:, SK, :], xT[:, idx, :])
                elif kind == "v":
                    for t in range(2):
                        last = mm(m[:, D * t:D * (t + 1)], xT[:, idx, 128 * t:128 * (t + 1)], aw[:, SV, :])
                elif kind == "ck":
                    pe.wait_ge(ld_aw2, 16)
                    wait_read(pe, ("cT", idx))
                    last = mm(m, aw[:, CK, :], cT[:, idx, :])
                elif kind == "cv":
                    for t in range(4):
                        last = mm(m[:, D * t:D * (t + 1)], cT[:, idx, 128 * t:128 * (t + 1)], aw[:, CV, :])
                elif kind == "cq":
                    wait_read(pe, ("yT", idx))
                    last = mm(m[:, 0:L], aw[:, CQ, :], yT[:, idx, :])
                elif kind == "m":
                    pe.wait_ge(negmax_ready, idx + 1)
                    pe.wait_ge(idb_ready, 1)
                    for q in range(QT):
                        last = nc.tensor.transpose(
                            m.bitcast(BF16)[0:2 * HALF, 128 * q:128 * (q + 1)],
                            negmax_parts[:, idx % 2, q].rearrange("p a h -> p (a h)"), idb[:, :])
                elif kind == "oT":
                    blk, qt = item[1:]
                    pe.wait_ge(av_read, 4 * (blk + 1))
                    for g in range(4):
                        last = nc.tensor.transpose(m[:, 128 * g:128 * (g + 1)],
                                                   av_sb[:, blk % 2, g, 128 * qt:128 * (qt + 1)], idf[:, :])
                elif kind == "aT":
                    wait_read(pe, ("oT", idx, 0))
                    wait_read(pe, ("oT", idx, 1))
                    for q in range(QT):
                        last = nc.tensor.transpose(m[:, 128 * q:128 * (q + 1)], attn[:, q, :], idf[:, :])
                elif kind == "op":
                    wait_read(pe, ("aT", idx))
                    w = aw[:, SO if idx < 2 else CO, :]
                    for q in range(QT):
                        last = mm(m[:, D * q:D * (q + 1)], attnT[:, 128 * q:128 * (q + 1)], w)
                elif kind == "rt":
                    pe.wait_ge(ld_rw, 16)
                    wait_read(pe, ("wT", idx))
                    for q in range(QT):
                        last = mm(m[:, E * q:E * (q + 1)], wT[:, idx, 128 * q:128 * (q + 1)], rw_sb[:, :])
                elif kind == "gT":
                    pe.wait_ge(gates_ready, idx + 1)
                    for q in range(QT):
                        last = nc.tensor.transpose(m[0:E, 128 * q:128 * (q + 1)], gates[:, idx, q, :], idf[:, :])
                elif kind == "b2":
                    pe.wait_ge(ld_b2, 16)
                    wait_read(pe, ("gT", idx))
                    for q in range(QT):
                        last = mm(m[:, D * q:D * (q + 1)], gatesT[:, idx, 128 * q:128 * (q + 1)], b2_sb[:, :])
                last.then_inc(misc_full[bank(item)], 1)

            def operands(i):
                blk, b = i // 2, (i // 2) % 2
                return q_op[:, blk], (k_self[:, b] if blk < 2 else k_cross[:, b])

            def pass1(i, s):
                q, k = operands(i)
                if s == 0 and i % 2 == 0:
                    pe.wait_ge(q_ready[i // 2], 16 * 6)
                    pe.wait_ge(k_ready[i // 2], 16 * 3)
                for c in range(nkc(i) // 2):
                    n = BASE[i] + s * (nkc(i) // 2) + c
                    if n >= S1_BANKS:
                        pe.wait_ge(s1_read, n - S1_BANKS + 1)
                    dst = s1[:, n % S1_BANKS, :]
                    if i < 4:
                        qt = s % 2
                        for p in range(2):
                            h = HALF * (i % 2) + s - s % 2 + p
                            last = mm(dst[:, L * p:L * (p + 1)], q[:, h, 128 * qt:128 * (qt + 1)], k[:, h, :])
                    else:
                        h = HALF * (i % 2) + s
                        last = mm(dst, q[:, h, 128 * c:128 * (c + 1)], k[:, h, :])
                    last.then_inc(s1_full, 1)

            def pass2(i, s):
                q, k = operands(i)
                h = HALF * (i % 2) + s
                if s == 0:
                    pe.wait_ge(max_rows[i], 32)
                for c in range(nkc(i) // 2):
                    n = BASE[i] + s * (nkc(i) // 2) + c
                    if n >= S2_BANKS:
                        pe.wait_ge(probs_ready, n - S2_BANKS + 1)
                    for p in range(2):
                        kc = 2 * c + p
                        last = mm(s2[:, n % S2_BANKS, L * p:L * (p + 1)], k[:, h, 128 * kc:128 * (kc + 1)], q[:, h, :])
                    last.then_inc(s2_full, 1)

            def times_v(i, g):
                blk, b, a = i // 2, (i // 2) % 2, 2 * i + g
                v = v_self[:, b] if blk < 2 else v_cross[:, b]
                tiles = nkc(i) // 2
                wait_read(pe, ("v" if blk < 2 else "cv", b))
                pe.wait_ge(probs_ready, BASE[i] + 4 * (g + 1) * tiles)
                if a:
                    pe.wait_ge(av_read, a)
                for kc in range(nkc(i)):
                    for j in range(4):
                        n = BASE[i] + (4 * g + j) * tiles + kc // 2
                        h = HALF * (i % 2) + 4 * g + j
                        last = mm(avp[32 * j:32 * j + DH + 1, 0:L], v[:, kc, h, :],
                                  probs[:, n % NP_TILES, L * (kc % 2):L * (kc % 2 + 1)],
                                  start=kc == 0, stop=kc == nkc(i) - 1)
                last.then_inc(av_full, 1)

            def fc1(n):
                b, e = divmod(n, E)
                for cp in range(2):
                    f = 2 * n + cp
                    if f >= 4:
                        pe.wait_ge(gelu_ready, f - 3)
                    for q in range(2):
                        last = mm(fc1_ring[f % 4][:, L * q:L * (q + 1)], w1_sb[:, e, 2 * cp + q, :], wT[:, b, :])
                    last.then_inc(fc1_full, 1)

            def fc2(n):
                b, e = divmod(n, E)
                pe.wait_ge(gelu_ready, 2 * n + 2)
                if n >= 2:
                    pe.wait_ge(acc_step, n - 1)
                for q in range(QT):
                    for k in range(NC1):
                        hidden = probs[:, 2 * (n % 3) + k // 2, L * (k % 2) + 128 * q:L * (k % 2) + 128 * (q + 1)]
                        last = mm(fc2_ring[n % 2][:, D * q:D * (q + 1)], hidden, w2_sb[:, e, k, :],
                                  start=k == 0, stop=k == NC1 - 1)
                last.then_inc(fc2_full, 1)

            pe.wait_ge(ld_id, 16)
            pe.wait_ge(ld_aw, 16)
            pe.wait_ge(av_zero, 1)
            for item in AFTER[-1]:
                extra(item)
            for t in range(N_STEPS):
                if pass1_at(t):
                    pass1(*pass1_at(t))
                if pass2_at(t):
                    pass2(*pass2_at(t))
                if av_at(t):
                    times_v(*av_at(t))
                for item in AFTER[t]:
                    extra(item)
            pe.wait_ge(s1_read, BASE[8])
            pe.wait_ge(probs_ready, BASE[8])
            pe.wait_ge(av_read, 16)
            pe.wait_ge(ld_w1, 16)
            pe.wait_ge(ld_w2, 16)
            for n in range(B * E):
                fc1(n)
                if n:
                    fc2(n - 1)
                for item in AFTER[N_STEPS + n]:
                    extra(item)
            fc2(B * E - 1)


def kernel(**inputs):
    import numpy as np
    import concourse.bacc as bacc
    from concourse.bass_utils import run_bass_kernel_spmd

    a = {k.replace("L0_xattn_", ""): np.asarray(v) for k, v in inputs.items()}
    order = np.arange(D).reshape(H, DH).T.reshape(D)

    def qkvo(in_w, out_w):
        wq, wk, wv = in_w[0:D], in_w[D:2 * D], in_w[2 * D:]
        return [wq[order].T, wk[order].T, wv.T, out_w.T]

    attn_w = np.stack(qkvo(a["sa_in_w"], a["sa_out_w"]) + qkvo(a["ca_in_w"], a["ca_out_w"]), axis=1)
    sab, cab = a["sa_in_b"], a["ca_in_b"]
    cols = np.stack([a["sa_ln_g"], a["sa_ln_b"], a["ca_q_ln_g"], a["ca_q_ln_b"], a["ca_kv_ln_g"], a["ca_kv_ln_b"],
                     a["moe_ln_g"], a["moe_ln_b"], sab[0:D][order], sab[D:2 * D][order],
                     cab[0:D][order], cab[D:2 * D][order], *a["e_fc1_b"].reshape(E * NC1, D)], axis=1)
    rows = np.stack([sab[2 * D:], a["sa_out_b"], cab[2 * D:], a["ca_out_b"]])
    e = np.arange(E)
    host = {
        "x": a["x"].reshape(B * L, D),
        "ctx_in": a["ctx_1024"].reshape(B * S, D),
        "attn_w": attn_w,
        "cols": cols,
        "rows": rows,
        "rb": a["router_b"],
        "w1": a["e_fc1_w"].transpose(2, 0, 1).reshape(D, E, NC1, D),
        "w2": a["e_fc2_w"].reshape(E, D, NC1, D).transpose(3, 0, 2, 1),
        "rw": a["router_w"].T,
        "b2": a["e_fc2_b"],
        "ident": np.eye(128, dtype=np.float32),
        "tri": np.broadcast_to((e[None, :] < e[:, None]).astype(np.float32), (128, E, E)),
    }
    nc = bacc.Bacc("TRN2", target_bir_lowering=False, num_devices=1)
    arrays, args = {}, []
    for name, v in host.items():
        v = np.ascontiguousarray(v)
        arrays[name + "_dram"] = v
        args.append(nc.dram_tensor(name + "_dram", v.shape, mybir.dt.from_np(v.dtype), kind="ExternalInput").ap())
    out = nc.dram_tensor("out_dram", [B * L, D], F32, kind="ExternalOutput").ap()
    xattn_moe(nc, *args, out)
    r = run_bass_kernel_spmd(nc, [arrays], core_ids=[0])
    return r.results[0]["out_dram"].reshape(B, L, D)
```

```python
from contextlib import ExitStack

import concourse.bass as bass
from concourse import mybir

F32 = mybir.dt.float32
BF16 = mybir.dt.bfloat16
ALU = mybir.AluOpType
ACT = mybir.ActivationFunctionType
AXX = mybir.AxisListType.X

D, H, E, DFF, B = 128, 16, 8, 512, 2
DH = D // H
L, S = 256, 512
EPS = 1e-5
SCALE = DH ** -0.5
NC1 = DFF // D
QT = L // 128
NP_TILES = 16
S1_BANKS, S2_BANKS = 2, 3
SLOTS = 9
MAXROW = SLOTS * DH

(SA_G, SA_B, CQ_G, CQ_B, CKV_G, CKV_B, MOE_G, MOE_B, SA_BQ, SA_BK, CA_BQ, CA_BK, FC1_B) = range(13)
NCOLS = FC1_B + E * NC1
SQ, SK, SV, SO, CQ, CK, CV, CO = range(8)
SA_BV, SA_BO, CA_BV, CA_BO = range(4)

GAP = 6
LAG = 4


def nbk(u):
    return 1 if u < 4 else 2


def pass1_start(u):
    return 8 * u + (GAP if u >= 4 else 0)


def pass2_start(u):
    return pass1_start(u) + 8 + LAG


N_STEPS = pass2_start(7) + 8 + 2
BASE = [0, 8, 16, 24, 32, 48, 64, 80, 96]

AFTER = {t: [] for t in range(-1, N_STEPS + 17)}
AFTER[-1] = [("xT", 0), ("qk", 0), ("xT", 1), ("qk", 1), ("v", 0), ("v", 1),
             ("cs", 0), ("cn", 0), ("cT", 0), ("ck", 0), ("cv", 0)]
for _u in range(8):
    AFTER[pass1_start(_u) + 8].append(("m", _u))
for _t, _x in ((31, ("cs", 1)), (32, ("cn", 1)), (33, ("cT", 1)), (34, ("ck", 1)), (35, ("cv", 1))):
    AFTER[_t].append(_x)
for _u in range(8):
    _t = pass2_start(_u) + 9
    for _k, _x in (((1, "oT"), (2, "aT"), (3, "op"), (5, "yn"), (6, "yT"), (7, "cq")) if _u < 4 else
                   ((1, "oT"), (2, "aT"), (3, "op"), (4, "wn"), (4, "wT"), (5, "rt"), (6, "ex"), (6, "rg"),
                    (7, "gT"), (8, "b2"))):
        AFTER[_t + _k].append((_x, _u))
for _n in range(E * B):
    AFTER[N_STEPS + _n].append(("e", _n))

MISC = {x: n for n, x in enumerate(
    x for t in AFTER for x in AFTER[t] if x[0] not in ("cs", "cn", "yn", "wn", "ex", "rg", "e"))}
SPLITS = [x for x in MISC if x[0] in ("qk", "ck", "cq")]
NORMS = [("x", 0), ("x", 1)] + [
    {"cs": ("c", x[1]), "op": ("y" if x[1] < 4 else "w", x[1] % 4)}[x[0]]
    for t in AFTER for x in AFTER[t] if x[0] in ("cs", "op")]
NORM_TILES = {"x": QT, "c": S // 128, "y": 1, "w": 1}


def pass1_at(t):
    return next(((u, t - pass1_start(u)) for u in range(8) if 0 <= t - pass1_start(u) < 8), None)


def pass2_at(t):
    return next(((u, t - pass2_start(u)) for u in range(8) if 0 <= t - pass2_start(u) < 8), None)


def av_at(t):
    return next(((u, g) for u in range(8) for g in range(4) if t == pass2_start(u) + 2 * g + 3), None)


def xattn_moe(nc, x, ctx_in, attn_w, cols, rows, rb, w1, w2, rw, b2, ident, tri, out):
    with ExitStack() as stack:
        def sb(name, shape, dt=F32):
            return stack.enter_context(nc.sbuf_tensor(name, shape, dt))

        def ps(name, shape, dt=F32):
            return stack.enter_context(nc.psum_tensor(name, shape, dt))

        def sem(name):
            return stack.enter_context(nc.semaphore(name))

        x_sb = sb("x_sb", [128, B * QT, D])
        c_sb = sb("c_sb", [128, B * 4, D])
        aw = sb("aw", [128, 8, D])
        col = sb("col", [128, NCOLS])
        row = sb("row", [128, 4, D])
        rb_bc = sb("rb_bc", [128, E])
        w1_sb = sb("w1_sb", [128, E, NC1, D])
        w2_sb = sb("w2_sb", [128, E, NC1, D])
        rw_sb = sb("rw_sb", [128, E])
        b2_sb = sb("b2_sb", [E, D])
        idf = sb("idf", [128, 128])
        idb = sb("idb", [128, 128], BF16)
        tri_sb = sb("tri_sb", [128, E, E])
        stats = sb("stats", [128, 4, 6])
        mv = sb("mv", [128, len(NORMS), 4, 2])
        veps = sb("veps", [128, len(NORMS), 4])
        rstd = sb("rstd", [128, len(NORMS), 4])
        mhalf = sb("mhalf", [128, 4])
        z_lat = sb("z_lat", [128, B * QT, D])
        zx = zy = z_lat
        zc = c_sb
        xT = sb("xT", [128, B, L])
        cT = sb("cT", [128, B, S])
        yT = wT = xT
        v_self = sb("v_self", [128, B, 2, H, DH + 1])
        v_cross = sb("v_cross", [128, B, 4, H, DH + 1])
        part_q = sb("part_q", [128, 2 * B, 3, 128], BF16)
        part_k = sb("part_k", [128, B, 3, S], BF16)
        part_ks, part_kc = part_k[:, :, :, 0:L], part_k
        rest = sb("rest", [128, 512])
        q_op = sb("q_op", [128, 8, H, 128], BF16)
        k_self = sb("k_self", [128, B, H, L], BF16)
        k_cross = sb("k_cross", [128, B, H, S], BF16)
        negmax = sb("negmax", [128, 2, H])
        negmax_parts = sb("negmax_parts", [128, 2, 2, H], BF16)
        negmaxT = sb("negmaxT", [2 * H, 2, 128], BF16)
        probs = sb("probs", [128, NP_TILES, 512])
        av_sb = sb("av_sb", [128, 4, 128])
        rsum = sb("rsum", [128, H])
        attn = sb("attn", [128, D])
        attnT = sb("attnT", [128, 128])
        res = sb("res", [128, B * QT, D])
        x1 = sb("x1", [128, B * QT, D])
        res2 = res
        x2 = x1
        lg = sb("lg", [128, E])
        top = sb("top", [128, 1])
        above = sb("above", [128, E, E])
        ties = sb("ties", [128, E, E])
        rank = sb("rank", [128, E])
        shifted = sb("shifted", [128, E])
        ex = sb("ex", [128, E])
        den = sb("den", [128, 1])
        gates = sb("gates", [128, 2 * B, E])
        gatesT = sb("gatesT", [E, 2 * B, 128])
        warm = sb("warm", [128, 1])
        acc = x1

        s1 = ps("s1", [128, S1_BANKS, 512])
        s2 = ps("s2", [128, S2_BANKS, 512])
        avp = ps("avp", [128, 512])
        misc = ps("misc", [128, 2, 512])
        fc1_ring = [s1[:, 0, :], s1[:, 1, :], s2[:, 0, :], s2[:, 1, :]]
        fc2_ring = [avp[:, :], s2[:, 2, :]]

        scr_q = nc.dram_tensor("scr_q", [8, 3, D, 128], BF16, kind="Internal").ap()
        scr_ks = nc.dram_tensor("scr_ks", [B, 3, D, L], BF16, kind="Internal").ap()
        scr_kc = nc.dram_tensor("scr_kc", [B, 3, D, S], BF16, kind="Internal").ap()

        ld_x = [sem(f"ld_x{b}") for b in range(B)]
        ld_c = [sem(f"ld_c{b}") for b in range(B)]
        ld_aw, ld_aw2, ld_col, ld_row, ld_rb = sem("ld_aw"), sem("ld_aw2"), sem("ld_col"), sem("ld_row"), sem("ld_rb")
        ld_w1, ld_w2, ld_rw, ld_b2 = sem("ld_w1"), sem("ld_w2"), sem("ld_rw"), sem("ld_b2")
        ld_id, ld_tri = sem("ld_id"), sem("ld_tri")
        idb_ready, mhalf_ready, v_ones, av_zero = sem("idb_ready"), sem("mhalf_ready"), sem("v_ones"), sem("av_zero")
        q_wiped = [sem(f"q_wiped{u}") for u in range(8)]
        k_wiped = [sem(f"k_wiped{k}") for k in range(4)]
        var_ready, rstd_ready = sem("var_ready"), sem("rstd_ready")
        z_ready = {n: sem(f"z{n[0]}{n[1]}") for n in NORMS}
        misc_full = [sem(f"misc_full{k}") for k in range(2)]
        misc_read = [sem(f"misc_read{k}") for k in range(2)]
        hi_ready, parts_ready = sem("hi_ready"), sem("parts_ready")
        q_stored = [sem(f"q_stored{k}") for k in range(len(SPLITS))]
        k_stored = [sem(f"k_stored{k}") for k in range(len(SPLITS))]
        q_ready = [sem(f"q_ready{u}") for u in range(8)]
        k_ready = [sem(f"k_ready{k}") for k in range(4)]
        s1_full, s1_read = sem("s1_full"), sem("s1_read")
        negmax_ready = sem("negmax_ready")
        max_rows = [sem(f"max_rows{u}") for u in range(8)]
        s2_full, probs_ready = sem("s2_full"), sem("probs_ready")
        av_full, av_read = sem("av_full"), sem("av_read")
        res_ready, res2_ready = sem("res_ready"), sem("res2_ready")
        shifted_ready, ex_ready, gates_ready = sem("shifted_ready"), sem("ex_ready"), sem("gates_ready")
        fc1_full, gelu_ready, fc2_full, acc_step = sem("fc1_full"), sem("gelu_ready"), sem("fc2_full"), sem("acc_step")
        stored = sem("stored")
        dve_own = sem("dve_own")

        def bank(item):
            return MISC[item] % 2

        def wait_full(eng, item):
            eng.wait_ge(misc_full[bank(item)], MISC[item] // 2 + 1)

        def wait_free(eng, item):
            if MISC[item] // 2 > 0:
                eng.wait_ge(misc_read[bank(item)], MISC[item] // 2)

        def wait_read(eng, item):
            eng.wait_ge(misc_read[bank(item)], MISC[item] // 2 + 1)

        def parts_of(item):
            kind, idx = item
            tiles = lambda m: m[:, 0:L].rearrange("p (t c) -> p t c", c=128)
            if kind == "qk":
                return [(tiles, lambda t: part_q[:, QT * idx:QT * (idx + 1), t, :], SA_BQ),
                        (lambda m: m[:, L:2 * L], lambda t: part_ks[:, idx, t, :], SA_BK)]
            if kind == "ck":
                return [(lambda m: m[:, 0:S], lambda t: part_kc[:, idx, t, :], CA_BK)]
            return [(lambda m: m[:, 0:128], lambda t: part_q[:, idx, t, :], CA_BQ)]

        block = stack.enter_context(nc.Block())

        @block.sync
        def _(sp):
            tok = x.rearrange("(t p) d -> p t d", p=128)
            ctok = ctx_in.rearrange("(t p) d -> p t d", p=128)
            for b in range(B):
                sp.dma_start(x_sb[:, QT * b:QT * (b + 1), :], tok[:, QT * b:QT * (b + 1), :]).then_inc(ld_x[b], 16)
                if b == 0:
                    sp.dma_start(idf[:, :], ident).then_inc(ld_id, 16)
                    sp.dma_start(col[:, :], cols).then_inc(ld_col, 16)
                    sp.dma_start(aw[:, 0:4, :], attn_w[:, 0:4, :]).then_inc(ld_aw, 16)
            sp.dma_start(c_sb[:, 0:4, :], ctok[:, 0:4, :]).then_inc(ld_c[0], 16)
            sp.dma_start(row[:, :, :], rows.unsqueeze(0).broadcast_to([128, 4, D])).then_inc(ld_row, 16)
            sp.dma_start(aw[:, 4:8, :], attn_w[:, 4:8, :]).then_inc(ld_aw2, 16)
            experts_asked = 0
            for j, item in enumerate(SPLITS):
                kind, idx = item
                sp.wait_ge(parts_ready, j + 1)
                units = [QT * idx, QT * idx + 1] if kind == "qk" else [4 + idx] if kind == "cq" else []
                keys = {"qk": (scr_ks, part_ks, k_self, 0), "ck": (scr_kc, part_kc, k_cross, 2)}.get(kind)
                if keys:
                    scr, part, op, base = keys
                    sp.dma_start(scr[idx].rearrange("t p c -> p t c"), part[:, idx]).then_inc(k_stored[j], 16)
                if units:
                    first = units[0]
                    sp.dma_start(scr_q[first:first + len(units)].rearrange("u t p c -> p u t c"),
                                 part_q[:, first % 4:first % 4 + len(units)]).then_inc(q_stored[j], 16)
                if keys:
                    sp.wait_ge(k_stored[j], 16)
                    sp.wait_ge(k_wiped[base + idx], 1)
                    for t in range(3):
                        src = scr[idx, t].rearrange("(d h) c -> d (h c)", d=DH)
                        sp.dma_start(op[3 * DH * t:3 * DH * (t + 1), idx],
                                     src.unsqueeze(0).broadcast_to([3, DH, src.shape[-1]])
                                     ).then_inc(k_ready[base + idx], 16)
                for u in units:
                    sp.wait_ge(q_stored[j], 16)
                    sp.wait_ge(q_wiped[u], 1)
                    src = scr_q[u].rearrange("t (d h) c -> (t d) (h c)", d=DH)
                    sp.dma_start(q_op[0:MAXROW, u], src.unsqueeze(0).broadcast_to([3, 3 * DH, H * 128])
                                 ).then_inc(q_ready[u], 16)
                if kind == "ck" and idx == 0:
                    sp.dma_start(c_sb[:, 4:8, :], ctok[:, 4:8, :]).then_inc(ld_c[1], 16)
                    sp.dma_start(rb_bc[:, :], rb.unsqueeze(0).broadcast_to([128, E])).then_inc(ld_rb, 16)
                    sp.dma_start(tri_sb[:, :, :], tri).then_inc(ld_tri, 16)
                    sp.dma_start(rw_sb[:, :], rw).then_inc(ld_rw, 16)
                    sp.dma_start(b2_sb[:, :], b2).then_inc(ld_b2, 16)
                if kind == "cq":
                    for e in range(2 * idx, 2 * idx + 2):
                        sp.dma_start(w1_sb[:, e], w1[:, e]).then_inc(ld_w1, 16)
                        sp.dma_start(w2_sb[:, e], w2[:, e]).then_inc(ld_w2, 16)
            out_t = out.rearrange("(t p) d -> p t d", p=128)
            for b in range(B):
                sp.wait_ge(acc_step, E * (b + 1))
                sp.dma_start(out_t[:, QT * b:QT * (b + 1), :], acc[:, QT * b:QT * (b + 1), :]).then_inc(stored, 16)
            sp.wait_ge(stored, 16 * B)

        @block.gpsimd
        def _(pool):
            def power(n):
                w = NORM_TILES[NORMS[n][0]]
                pool.wait_ge(var_ready, n + 1)
                nc.gpsimd.tensor_tensor(rstd[:, n, 0:w], veps[:, n, 0:w], mhalf[:, 0:w], ALU.pow).then_inc(rstd_ready, 1)

            def wipe_q(u):
                nc.gpsimd.memset(q_op[:, u], 0.0).then_inc(q_wiped[u], 1)

            def wipe_k(blk):
                nc.gpsimd.memset(k_self[:, blk] if blk < 2 else k_cross[:, blk - 2], 1.0).then_inc(k_wiped[blk], 1)

            nc.gpsimd.memset(mhalf[:, :], -0.5).then_inc(mhalf_ready, 1)
            wipe_k(0)
            pool.wait_ge(mhalf_ready, 1)
            power(0)
            power(1)
            wipe_q(1)
            nc.gpsimd.memset(v_self[:], 1.0)
            nc.gpsimd.memset(v_cross[:], 1.0).then_inc(v_ones, 1)
            wipe_k(1)
            wipe_q(2)
            power(2)
            wipe_q(3)
            wipe_k(2)
            pool.wait_ge(ld_row, 16)
            for b in range(B):
                pool.wait_ge(ld_x[b], 16)
            for t in range(B * QT):
                last = nc.gpsimd.tensor_tensor(res[:, t, :], x_sb[:, t, :], row[:, SA_BO, :], ALU.add)
            last.then_inc(res_ready, 1)
            wipe_q(4)
            wipe_q(5)
            for n in range(3, len(NORMS)):
                name, idx = NORMS[n]
                power(n)
                if name == "c":
                    wipe_k(3)
                elif name == "y":
                    wait_read(pool, ("op", idx))
                    nc.gpsimd.tensor_tensor(res2[:, idx, :], x1[:, idx, :], row[:, CA_BO, :], ALU.add).then_inc(res2_ready, 1)
                    if idx < 2:
                        wipe_q(6 + idx)

        @block.scalar
        def _(act):
            def identity(dst, src, bias, scale=1.0):
                return nc.scalar.activation(dst, src, ACT.Identity, bias=bias, scale=scale)

            def c(j):
                return col[:, j:j + 1]

            def extra(item):
                kind, idx = item[0], item[1]
                if kind == "ex":
                    act.wait_ge(shifted_ready, idx - 3)
                    nc.scalar.activation(ex[:, :], shifted[:, :], ACT.Exp).then_inc(ex_ready, 1)
                elif kind == "e":
                    gelus(idx)
                if kind in ("cs", "cn", "yn", "wn", "rt", "ex", "rg", "v", "cv", "op", "oT", "b2", "e"):
                    return
                wait_full(act, item)
                m = misc[:, bank(item), :]
                free = misc_read[bank(item)]
                if kind == "xT":
                    identity(xT[:, idx, :], m[:, 0:L], c(SA_B), c(SA_G)).then_inc(free, 1)
                elif kind == "cT":
                    identity(cT[:, idx, :], m[:, 0:S], c(CKV_B), c(CKV_G)).then_inc(free, 1)
                elif kind == "yT":
                    identity(yT[:, idx // 2, 128 * (idx % 2):128 * (idx % 2 + 1)], m[:, 0:128], c(CQ_B), c(CQ_G)).then_inc(free, 1)
                elif kind == "wT":
                    identity(wT[:, idx // 2 - 2, 128 * (idx % 2):128 * (idx % 2 + 1)], m[:, 0:128], c(MOE_B), c(MOE_G)).then_inc(free, 1)
                elif kind in ("qk", "ck", "cq"):
                    if kind == "ck":
                        act.wait_ge(k_stored[SPLITS.index(("qk", idx))], 16)
                    elif kind == "cq":
                        act.wait_ge(q_stored[SPLITS.index(("qk", idx // 2))], 16)
                    for view, part, bias in parts_of(item):
                        last = identity(part(0), view(m), c(bias))
                    last.then_inc(hi_ready, 1)
                elif kind == "aT":
                    nc.scalar.copy(attnT[:, :], m[:, 0:128]).then_inc(free, 1)
                elif kind == "gT":
                    nc.scalar.copy(gatesT[:, idx - 4, :], m[0:E, 0:128]).then_inc(free, 1)
                elif kind == "m":
                    u = idx
                    if u >= 2:
                        act.wait_ge(max_rows[u - 2], 16)
                    nc.scalar.copy(negmaxT[:, u % 2, :], m.bitcast(BF16)[0:2 * H, 0:128]).then_inc(free, 1)
                    wait_read(act, item)
                    act.dma_start(q_op[MAXROW:MAXROW + 2, u, :, :], negmaxT[:, u % 2, :]).then_inc(max_rows[u], 16)

            def gelus(n):
                e = n % E
                for cp in range(2):
                    act.wait_ge(fc1_full, 2 * n + cp + 1)
                    if n >= 3 and cp == 0:
                        act.wait_ge(fc2_full, n - 2)
                    for q in range(2):
                        k = 2 * cp + q
                        last = nc.scalar.activation(
                            probs[:, 2 * (n % 3) + cp, L * q:L * (q + 1)], fc1_ring[(2 * n + cp) % 4][:, L * q:L * (q + 1)],
                            ACT.Gelu, bias=c(FC1_B + e * NC1 + k))
                    last.then_inc(gelu_ready, 1)

            act.wait_ge(mhalf_ready, 1)
            nc.scalar.activation(warm[:, :], mhalf[:, 0:1], ACT.Exp)
            act.wait_ge(ld_col, 16)
            for item in AFTER[-1]:
                extra(item)
            for t in range(N_STEPS + B * E):
                if pass2_at(t):
                    u, s = pass2_at(t)
                    for k in range(nbk(u)):
                        n = BASE[u] + s * nbk(u) + k
                        act.wait_ge(s2_full, n + 1)
                        if n >= NP_TILES:
                            old = n - NP_TILES
                            ou = max(q for q in range(8) if BASE[q] <= old)
                            act.wait_ge(av_full, 4 * ou + (old - BASE[ou]) // (2 * nbk(ou)) + 1)
                        nc.scalar.activation(probs[:, n % NP_TILES, :], s2[:, n % S2_BANKS, :], ACT.Exp,
                                             scale=SCALE).then_inc(probs_ready, 1)
                if av_at(t) and av_at(t)[1] == 3:
                    u = av_at(t)[0]
                    act.wait_ge(av_full, 4 * (u + 1))
                    if u:
                        wait_full(act, ("oT", u - 1))
                    nc.scalar.copy(av_sb[:, :, :], avp[:, :].rearrange("p (g c) -> p g c", c=128)).then_inc(av_read, 1)
                for item in AFTER[t]:
                    extra(item)

        @block.vector
        def _(dve):
            own = [0]

            def link(ins):
                own[0] += 1
                ins.then_inc(dve_own, 1)
                dve.wait_ge(dve_own, own[0])

            def norm_stats(name, src):
                n, w = NORMS.index(name), NORM_TILES[name[0]]
                for t in range(w):
                    last = nc.vector.bn_stats(stats[:, t, :], src[:, t, :])
                link(last)
                for t in range(w):
                    last = nc.vector.bn_aggr(mv[:, n, t, :], stats[:, t, :])
                link(last)
                nc.vector.tensor_scalar_add(veps[:, n, 0:w], mv[:, n, 0:w, 1], EPS).then_inc(var_ready, 1)

            def norm(name, src, z):
                n, w = NORMS.index(name), NORM_TILES[name[0]]
                dve.wait_ge(rstd_ready, n + 1)
                for t in range(w):
                    last = nc.vector.tensor_scalar(z[:, t, :], src[:, t, :], mv[:, n, t, 0:1], rstd[:, n, t:t + 1],
                                                   ALU.subtract, ALU.mult)
                last.then_inc(z_ready[name], 1)

            def negmax_split(u):
                dve.wait_ge(s1_read, BASE[u + 1])
                if u >= 2:
                    wait_full(dve, ("m", u - 2))
                link(nc.vector.tensor_copy(negmax_parts[:, u % 2, 0, :], negmax[:, u % 2]))
                nc.vector.tensor_tensor(negmax_parts[:, u % 2, 1, :], negmax[:, u % 2],
                                        negmax_parts[:, u % 2, 0, :], ALU.subtract).then_inc(negmax_ready, 1)

            def split(item):
                j = SPLITS.index(item)
                m = misc[:, bank(item), :]
                wait_full(dve, item)
                dve.wait_ge(hi_ready, j + 1)
                for view, part, bias in parts_of(item):
                    last = nc.vector.scalar_tensor_tensor(view(rest), view(m), col[:, bias:bias + 1], part(0),
                                                          ALU.add, ALU.subtract)
                last.then_inc(misc_read[bank(item)], 1)
                wait_read(dve, item)
                for view, part, bias in parts_of(item):
                    last = nc.vector.tensor_copy(part(1), view(rest))
                link(last)
                for view, part, bias in parts_of(item):
                    last = nc.vector.tensor_tensor(part(2), view(rest), part(1), ALU.subtract)
                last.then_inc(parts_ready, 1)
                dve.wait_ge(parts_ready, j + 1)

            def values(item, v, bias):
                w = 2 if item[0] == "v" else 4
                wait_full(dve, item)
                for t in range(w):
                    last = nc.vector.tensor_tensor(
                        v[:, t, :, 0:DH], misc[:, bank(item), D * t:D * (t + 1)].rearrange("p (h d) -> p h d", d=DH),
                        row[:, bias, :].rearrange("p (h d) -> p h d", d=DH), ALU.add)
                last.then_inc(misc_read[bank(item)], 1)

            def rank_logits(item):
                wait_full(dve, item)
                nc.vector.tensor_tensor(lg[:, :], misc[:, bank(item), 0:E], rb_bc[:, :], ALU.add).then_inc(misc_read[bank(item)], 1)
                wait_read(dve, item)
                link(nc.vector.tensor_reduce(top[:, :], lg[:, :], AXX, ALU.max))
                nc.vector.tensor_scalar(shifted[:, :], lg[:, :], top[:, 0:1], None, ALU.subtract).then_inc(shifted_ready, 1)
                mine = lg[:, :].unsqueeze(2).broadcast_to([128, E, E])
                others = lg[:, :].unsqueeze(1).broadcast_to([128, E, E])
                link(nc.vector.tensor_tensor(ties[:, :, :], others, mine, ALU.is_equal))
                nc.vector.tensor_tensor(above[:, :, :], others, mine, ALU.is_gt)
                link(nc.vector.tensor_tensor(ties[:, :, :], ties[:, :, :], tri_sb[:, :, :], ALU.mult))
                link(nc.vector.tensor_tensor(above[:, :, :], above[:, :, :], ties[:, :, :], ALU.add))
                link(nc.vector.tensor_reduce(rank[:, :], above[:, :, :], AXX, ALU.add))

            def set_gates(u):
                dve.wait_ge(ex_ready, u - 3)
                link(nc.vector.scalar_tensor_tensor(rank[:, :], rank[:, :], 1.5, ex[:, :], ALU.is_lt, ALU.mult))
                link(nc.vector.tensor_reduce(den[:, :], rank[:, :], AXX, ALU.add))
                link(nc.vector.reciprocal(den[:, :], den[:, :]))
                nc.vector.tensor_scalar(gates[:, u - 4, :], rank[:, :], den[:, 0:1], None, ALU.mult).then_inc(gates_ready, 1)
                dve.wait_ge(gates_ready, u - 3)

            def add_expert(n):
                b, e = divmod(n, E)
                dve.wait_ge(fc2_full, n + 1)
                for q in range(QT):
                    t = QT * b + q
                    last = nc.vector.scalar_tensor_tensor(acc[:, t, :], fc2_ring[n % 2][:, D * q:D * (q + 1)],
                                                          gates[:, t, e:e + 1], acc[:, t, :], ALU.mult, ALU.add)
                last.then_inc(acc_step, 1)
                dve.wait_ge(acc_step, n + 1)

            def extra(item):
                kind, idx = item[0], item[1]
                if kind == "cs":
                    dve.wait_ge(ld_c[idx], 16)
                    norm_stats(("c", idx), c_sb[:, 4 * idx:4 * idx + 4, :])
                elif kind == "cn":
                    norm(("c", idx), c_sb[:, 4 * idx:4 * idx + 4, :], zc[:, 4 * idx:4 * idx + 4, :])
                elif kind in ("qk", "ck", "cq"):
                    split(item)
                elif kind == "v":
                    dve.wait_ge(ld_row, 16)
                    dve.wait_ge(v_ones, 1)
                    values(item, v_self[:, idx], SA_BV)
                elif kind == "cv":
                    values(item, v_cross[:, idx], CA_BV)
                elif kind == "oT":
                    wait_full(dve, item)
                    o = misc[:, bank(item), :].rearrange("p (h c) -> p h c", c=32)
                    link(nc.vector.reciprocal(rsum[:, :], o[:, :, DH]))
                    if idx:
                        wait_full(dve, ("aT", idx - 1))
                    nc.vector.tensor_tensor(attn[:, :].rearrange("p (h d) -> p h d", d=DH), o[:, :, 0:DH],
                                            rsum[:, :].unsqueeze(2).broadcast_to([128, H, DH]),
                                            ALU.mult).then_inc(misc_read[bank(item)], 1)
                    wait_read(dve, item)
                elif kind == "op":
                    wait_full(dve, item)
                    t = idx % 4
                    if idx < 4:
                        dve.wait_ge(res_ready, 1)
                    else:
                        dve.wait_ge(res2_ready, t + 1)
                    nc.vector.tensor_tensor(x1[:, t, :], misc[:, bank(item), 0:128], res[:, t, :],
                                            ALU.add).then_inc(misc_read[bank(item)], 1)
                    wait_read(dve, item)
                    norm_stats(("y" if idx < 4 else "w", t), x1[:, t:t + 1, :])
                elif kind == "yn":
                    norm(("y", idx), x1[:, idx:idx + 1, :], zy[:, idx:idx + 1, :])
                elif kind == "wn":
                    t = idx - 4
                    norm(("w", t), x2[:, t:t + 1, :], zx[:, t:t + 1, :])
                elif kind == "rt":
                    if idx == 4:
                        dve.wait_ge(ld_rb, 16)
                        dve.wait_ge(ld_tri, 16)
                    rank_logits(item)
                elif kind == "rg":
                    set_gates(idx)
                elif kind == "b2":
                    wait_full(dve, item)
                    t = idx - 4
                    nc.vector.tensor_tensor(acc[:, t, :], misc[:, bank(item), 0:D], x2[:, t, :],
                                            ALU.add).then_inc(misc_read[bank(item)], 1)
                    wait_read(dve, item)
                elif kind == "e" and idx:
                    add_expert(idx - 1)

            nc.vector.memset(avp[:, :], 0.0).then_inc(av_zero, 1)
            nc.vector.memset(q_op[:, 0], 0.0).then_inc(q_wiped[0], 1)
            for b in range(B):
                dve.wait_ge(ld_x[b], 16)
                norm_stats(("x", b), x_sb[:, QT * b:QT * (b + 1), :])
                if b == 0:
                    dve.wait_ge(ld_id, 16)
                    nc.vector.tensor_copy(idb[:, :], idf[:, :]).then_inc(idb_ready, 1)
                    norm(("x", b), x_sb[:, QT * b:QT * (b + 1), :], zx[:, QT * b:QT * (b + 1), :])
            norm(("x", 1), x_sb[:, QT:2 * QT, :], zx[:, QT:2 * QT, :])
            dve.wait_ge(ld_col, 16)
            for item in AFTER[-1]:
                extra(item)
            for t in range(N_STEPS + B * E):
                for item in AFTER[t]:
                    if item[0] == "m":
                        negmax_split(item[1])
                if pass1_at(t):
                    u, s = pass1_at(t)
                    for k in range(nbk(u)):
                        n = BASE[u] + s * nbk(u) + k
                        dve.wait_ge(s1_full, n + 1)
                        if nbk(u) == 1:
                            dst = negmax[:, u % 2, 2 * s:2 * s + 2]
                            src = s1[:, n % S1_BANKS, :].rearrange("p (h k) -> p h k", h=2)
                        else:
                            dst = negmax[:, u % 2, 2 * s + k:2 * s + k + 1]
                            src = s1[:, n % S1_BANKS, :]
                        nc.vector.tensor_reduce(dst, src, AXX, ALU.max, negate=True).then_inc(s1_read, 1)
                for item in AFTER[t]:
                    extra(item)
            add_expert(B * E - 1)

        @block.tensor
        def _(pe):
            def mm(dst, lhsT, rhs, start=True, stop=True):
                return nc.tensor.matmul(dst, lhsT, rhs, start=start, stop=stop)

            def extra(item):
                kind, idx = item[0], item[1]
                if kind in ("cs", "cn", "yn", "wn", "ex", "rg"):
                    return
                if kind == "e":
                    fc1(idx)
                    if idx:
                        fc2(idx - 1)
                    return
                m = misc[:, bank(item), :]
                wait_free(pe, item)
                if kind in ("xT", "cT", "yT", "wT"):
                    name = (kind[0], idx % 4 if kind == "wT" else idx)
                    z = zc if kind == "cT" else z_lat
                    w = NORM_TILES[kind[0]]
                    pe.wait_ge(z_ready[name], 1)
                    for t in range(w):
                        last = nc.tensor.transpose(m[:, 128 * t:128 * (t + 1)], z[:, w * name[1] + t, :], idf[:, :])
                elif kind == "qk":
                    wait_read(pe, ("xT", idx))
                    mm(m[:, 0:L], aw[:, SQ, :], xT[:, idx, :])
                    last = mm(m[:, L:2 * L], aw[:, SK, :], xT[:, idx, :])
                elif kind == "v":
                    for t in range(2):
                        last = mm(m[:, D * t:D * (t + 1)], xT[:, idx, 128 * t:128 * (t + 1)], aw[:, SV, :])
                elif kind == "ck":
                    pe.wait_ge(ld_aw2, 16)
                    wait_read(pe, ("cT", idx))
                    last = mm(m, aw[:, CK, :], cT[:, idx, :])
                elif kind == "cv":
                    for t in range(4):
                        last = mm(m[:, D * t:D * (t + 1)], cT[:, idx, 128 * t:128 * (t + 1)], aw[:, CV, :])
                elif kind == "cq":
                    wait_read(pe, ("yT", idx))
                    last = mm(m[:, 0:128], aw[:, CQ, :], yT[:, idx // 2, 128 * (idx % 2):128 * (idx % 2 + 1)])
                elif kind == "m":
                    pe.wait_ge(negmax_ready, idx + 1)
                    pe.wait_ge(idb_ready, 1)
                    last = nc.tensor.transpose(m.bitcast(BF16)[0:2 * H, 0:128],
                                               negmax_parts[:, idx % 2].rearrange("p a h -> p (a h)"), idb[:, :])
                elif kind == "oT":
                    pe.wait_ge(av_read, idx + 1)
                    for g in range(4):
                        last = nc.tensor.transpose(m[:, 128 * g:128 * (g + 1)], av_sb[:, g, :], idf[:, :])
                elif kind == "aT":
                    wait_read(pe, ("oT", idx))
                    last = nc.tensor.transpose(m[:, 0:128], attn[:, :], idf[:, :])
                elif kind == "op":
                    wait_read(pe, ("aT", idx))
                    last = mm(m[:, 0:D], attnT[:, :], aw[:, SO if idx < 4 else CO, :])
                elif kind == "rt":
                    pe.wait_ge(ld_rw, 16)
                    wait_read(pe, ("wT", idx))
                    last = mm(m[:, 0:E], wT[:, idx // 2 - 2, 128 * (idx % 2):128 * (idx % 2 + 1)], rw_sb[:, :])
                elif kind == "gT":
                    pe.wait_ge(gates_ready, idx - 3)
                    last = nc.tensor.transpose(m[0:E, 0:128], gates[:, idx - 4, :], idf[:, :])
                elif kind == "b2":
                    pe.wait_ge(ld_b2, 16)
                    wait_read(pe, ("gT", idx))
                    last = mm(m[:, 0:D], gatesT[:, idx - 4, :], b2_sb[:, :])
                last.then_inc(misc_full[bank(item)], 1)

            def keys(u):
                return k_self[:, u // 2] if u < 4 else k_cross[:, u // 2 - 2]

            def pass1(u, s):
                k = keys(u)
                if s == 0:
                    pe.wait_ge(q_ready[u], 16)
                    pe.wait_ge(k_ready[u // 2], 16 * 3)
                for p in range(2):
                    h = 2 * s + p
                    n = BASE[u] + s * nbk(u) + (p if nbk(u) == 2 else 0)
                    if n >= S1_BANKS and (p == 0 or nbk(u) == 2):
                        pe.wait_ge(s1_read, n - S1_BANKS + 1)
                    if nbk(u) == 1:
                        last = mm(s1[:, n % S1_BANKS, L * p:L * (p + 1)], q_op[:, u, h, :], k[:, h, :])
                        if p == 1:
                            last.then_inc(s1_full, 1)
                    else:
                        mm(s1[:, n % S1_BANKS, :], q_op[:, u, h, :], k[:, h, :]).then_inc(s1_full, 1)

            def pass2(u, s):
                k, chunks = keys(u), 2 * nbk(u)
                if s == 0:
                    pe.wait_ge(max_rows[u], 16)
                for p in range(2):
                    h = 2 * s + p
                    n = BASE[u] + s * nbk(u) + (p if nbk(u) == 2 else 0)
                    if n >= S2_BANKS and (p == 0 or nbk(u) == 2):
                        pe.wait_ge(probs_ready, n - S2_BANKS + 1)
                    for kc in range(chunks):
                        at = 128 * ((h * chunks + kc) % 4)
                        last = mm(s2[:, n % S2_BANKS, at:at + 128], k[:, h, 128 * kc:128 * (kc + 1)], q_op[:, u, h, :])
                    if p == 1 or nbk(u) == 2:
                        last.then_inc(s2_full, 1)

            def times_v(u, g):
                b, chunks = (u // 2) % 2, 2 * nbk(u)
                v = v_self[:, b] if u < 4 else v_cross[:, b]
                if g == 0:
                    wait_read(pe, ("v" if u < 4 else "cv", b))
                    if u:
                        pe.wait_ge(av_read, u)
                pe.wait_ge(probs_ready, BASE[u] + 2 * (g + 1) * nbk(u))
                for kc in range(chunks):
                    for j in range(4):
                        h = 4 * g + j
                        n = BASE[u] + (h * chunks + kc) // 4
                        at = 128 * ((h * chunks + kc) % 4)
                        last = mm(avp[32 * j:32 * j + DH + 1, 128 * g:128 * (g + 1)], v[:, kc, h, :],
                                  probs[:, n % NP_TILES, at:at + 128], start=kc == 0, stop=kc == chunks - 1)
                last.then_inc(av_full, 1)

            def fc1(n):
                b, e = divmod(n, E)
                if n == 0:
                    pe.wait_ge(s1_read, BASE[8])
                    pe.wait_ge(probs_ready, BASE[8])
                    pe.wait_ge(av_read, 8)
                    pe.wait_ge(ld_w1, 16 * E)
                    pe.wait_ge(ld_w2, 16 * E)
                for cp in range(2):
                    f = 2 * n + cp
                    if f >= 4:
                        pe.wait_ge(gelu_ready, f - 3)
                    for q in range(2):
                        last = mm(fc1_ring[f % 4][:, L * q:L * (q + 1)], w1_sb[:, e, 2 * cp + q, :], wT[:, b, :])
                    last.then_inc(fc1_full, 1)

            def fc2(n):
                b, e = divmod(n, E)
                pe.wait_ge(gelu_ready, 2 * n + 2)
                if n >= 2:
                    pe.wait_ge(acc_step, n - 1)
                for q in range(QT):
                    for k in range(NC1):
                        hidden = probs[:, 2 * (n % 3) + k // 2, L * (k % 2) + 128 * q:L * (k % 2) + 128 * (q + 1)]
                        last = mm(fc2_ring[n % 2][:, D * q:D * (q + 1)], hidden, w2_sb[:, e, k, :],
                                  start=k == 0, stop=k == NC1 - 1)
                last.then_inc(fc2_full, 1)

            pe.wait_ge(ld_id, 16)
            pe.wait_ge(ld_aw, 16)
            pe.wait_ge(av_zero, 1)
            for item in AFTER[-1]:
                extra(item)
            for t in range(N_STEPS + B * E):
                if pass1_at(t):
                    pass1(*pass1_at(t))
                if pass2_at(t):
                    pass2(*pass2_at(t))
                if av_at(t):
                    times_v(*av_at(t))
                for item in AFTER[t]:
                    extra(item)
            fc2(B * E - 1)


def kernel(**inputs):
    import numpy as np
    import concourse.bacc as bacc
    from concourse.bass_utils import run_bass_kernel_spmd

    a = {k.replace("L0_xattn_", ""): np.asarray(v) for k, v in inputs.items()}
    order = np.arange(D).reshape(H, DH).T.reshape(D)

    def qkvo(in_w, out_w):
        wq, wk, wv = in_w[0:D], in_w[D:2 * D], in_w[2 * D:]
        return [wq[order].T, wk[order].T, wv.T, out_w.T]

    attn_w = np.stack(qkvo(a["sa_in_w"], a["sa_out_w"]) + qkvo(a["ca_in_w"], a["ca_out_w"]), axis=1)
    sab, cab = a["sa_in_b"], a["ca_in_b"]
    cols = np.stack([a["sa_ln_g"], a["sa_ln_b"], a["ca_q_ln_g"], a["ca_q_ln_b"], a["ca_kv_ln_g"], a["ca_kv_ln_b"],
                     a["moe_ln_g"], a["moe_ln_b"], sab[0:D][order], sab[D:2 * D][order],
                     cab[0:D][order], cab[D:2 * D][order], *a["e_fc1_b"].reshape(E * NC1, D)], axis=1)
    rows = np.stack([sab[2 * D:], a["sa_out_b"], cab[2 * D:], a["ca_out_b"]])
    e = np.arange(E)
    host = {
        "x": a["x"].reshape(B * L, D),
        "ctx_in": a["ctx_1024"].reshape(B * S, D),
        "attn_w": attn_w,
        "cols": cols,
        "rows": rows,
        "rb": a["router_b"],
        "w1": a["e_fc1_w"].transpose(2, 0, 1).reshape(D, E, NC1, D),
        "w2": a["e_fc2_w"].reshape(E, D, NC1, D).transpose(3, 0, 2, 1),
        "rw": a["router_w"].T,
        "b2": a["e_fc2_b"],
        "ident": np.eye(128, dtype=np.float32),
        "tri": np.broadcast_to((e[None, :] < e[:, None]).astype(np.float32), (128, E, E)),
    }
    nc = bacc.Bacc("TRN2", target_bir_lowering=False, num_devices=1)
    arrays, args = {}, []
    for name, v in host.items():
        v = np.ascontiguousarray(v)
        arrays[name + "_dram"] = v
        args.append(nc.dram_tensor(name + "_dram", v.shape, mybir.dt.from_np(v.dtype), kind="ExternalInput").ap())
    out = nc.dram_tensor("out_dram", [B * L, D], F32, kind="ExternalOutput").ap()
    xattn_moe(nc, *args, out)
    r = run_bass_kernel_spmd(nc, [arrays], core_ids=[0])
    return r.results[0]["out_dram"].reshape(B, L, D)
```

```python
from contextlib import ExitStack

import numpy as np

import concourse.bass as bass
from concourse import mybir

F32 = mybir.dt.float32
F32R = mybir.dt.float32r
BF16 = mybir.dt.bfloat16
ALU = mybir.AluOpType
ACT = mybir.ActivationFunctionType
AXX = mybir.AxisListType.X

D, H, E, DFF, B = 128, 16, 8, 512, 2
DH = D // H
L, S = 256, 512
EPS = 1e-5
SCALE = DH ** -0.5
NC1 = DFF // D
QT = L // 128
NP_TILES = 16
SLOTS = 9
ONES_PAIR = float(np.array([0x3F803F80], np.uint32).view(np.float32)[0])
MAXROW = SLOTS * DH

(SA_G, SA_B, CQ_G, CQ_B, CKV_G, CKV_B, MOE_G, MOE_B, SA_BQ, SA_BK, CA_BQ, CA_BK, SA_BV, CA_BV,
 FC1_B) = range(15)
NCOLS = FC1_B + E * NC1
SQ, SK, SV, SO, CQ, CK, CV, CO = range(8)
SA_BO, CA_BO = range(2)

PASS1 = (0, 16, 34, 50, 73, 89, 105, 121)
PASS2 = (26, 42, 60, 76, 96, 112, 128, 144)
M_LAG = 2
V_LAG = 4
CTX = ((12, 17, 29, 40, 43), (58, 72, 78, 86, 86))
OUT = (
    (22, 23, 24, 26, 29, 33),
    (23, 25, 28, 30, 32, 33),
    (22, 23, 26, 28, 30, 33),
    (23, 25, 27, 30, 31, 34),
    (21, 23, 25, 28, 31, 33, 37, 40, 43, 49),
    (21, 23, 25, 29, 30, 32, 36, 40, 42, 47),
    (21, 24, 26, 28, 29, 31, 34, 35, 37, 39),
    (21, 22, 24, 25, 25, 26, 27, 27, 28, 29),
)
DVE_LAG = {"ck": 2, "cv": 2, "cq": 1, "rt": 2, "wT": 2, "b2": 1}
S1_BANKS, S2_BANKS = 3, 2
STORE_LAG, FETCH_LAG = {"cm": 4, "cq": 4}, {"cm": 7, "cq": 7}
N_STEPS = PASS2[7] + 16 + V_LAG


def nbk(u):
    return 1 if u < 4 else 2


BASE = [0, 8, 16, 24, 32, 48, 64, 80, 96]

AFTER = {t: [] for t in range(-1, N_STEPS + 17)}
AFTER[-1] = [("xT", 0), ("sk", 0), ("sq", 0), ("xT", 1), ("sk", 1), ("sq", 1), ("v", 0), ("v", 1), ("cs", 0)]
for _u in range(8):
    AFTER[PASS1[_u] + 15 + M_LAG].append(("m", _u))
for _b in range(B):
    for _t, _x in zip(CTX[_b], ("cs", "cT", "ck", "cm", "cv")):
        if (_x, _b) != ("cs", 0):
            AFTER[_t].append((_x, _b))
for _u in range(8):
    for _t, _x in zip(OUT[_u], ("oT", "aT", "op", "yn", "yT", "cq") if _u < 4 else
                      ("oT", "aT", "op", "wn", "wT", "rt", "ex", "rg", "gT", "b2")):
        AFTER[PASS2[_u] + _t].append((_x, _u))
for _n in range(E * B):
    AFTER[N_STEPS + _n].append(("e", _n))
AFTER_DVE = {t: [x for s in AFTER for x in AFTER[s] if s + (DVE_LAG.get(x[0], 0) if 0 <= s < N_STEPS - 4 else 0) == t]
             for t in AFTER}

AFTER_SP = {t: [] for t in AFTER}
for _t in AFTER:
    for _x in AFTER[_t]:
        if _x[0] == "m":
            AFTER_SP[_t].append(("rows", _x))
        elif _x[0] in ("cm", "cq"):
            AFTER_SP[_t + STORE_LAG[_x[0]]].append(("store", ({"cm": "ck", "cq": "cq"}[_x[0]], _x[1])))
            AFTER_SP[_t + FETCH_LAG[_x[0]]].append(("fetch", ({"cm": "ck", "cq": "cq"}[_x[0]], _x[1])))

for _u in range(4, 8):
    _before = [x for t in AFTER_DVE for x in AFTER_DVE[t]]
    assert _before.index(("b2", _u)) < _before.index(("e", 1 + E * (_u // 2 - 2)))
    assert _before.index(("rg", _u)) < _before.index(("b2", _u))

MISC = {x: n for n, x in enumerate(
    x for t in AFTER for x in AFTER[t] if x[0] not in ("cs", "cm", "yn", "wn", "ex", "rg", "e"))}
SPLITS = [x for x in MISC if x[0] in ("sk", "sq", "ck", "cq")]
NORMS = [("x", 0), ("x", 1)] + [
    {"cs": ("c", x[1]), "op": ("y" if x[1] < 4 else "w", x[1] % 4)}[x[0]]
    for t in AFTER for x in AFTER[t] if x[0] in ("cs", "op")]
NORM_TILES = {"x": QT, "c": S // 128, "y": 1, "w": 1}


def pass2_bank(n):
    if n < BASE[7]:
        return S1_BANKS + n % S2_BANKS
    return n % (S1_BANKS + S2_BANKS)


def last_in_bank(n):
    return next((k for k in range(n - 1, -1, -1) if pass2_bank(k) == pass2_bank(n)), None)


def pass1_at(t):
    return next(((u, t - PASS1[u]) for u in range(8) if 0 <= t - PASS1[u] < H), None)


def pass2_at(t):
    return next(((u, t - PASS2[u]) for u in range(8) if 0 <= t - PASS2[u] < H), None)


def av_at(t):
    return next(((u, g) for u in range(8) for g in range(4) if t == PASS2[u] + 4 * g + 3 + V_LAG), None)


def xattn_moe(nc, x, ctx_in, attn_w, cols, rows, rb, w1, w2, rw, b2, ident, tri, out):
    with ExitStack() as stack:
        def sb(name, shape, dt=F32):
            return stack.enter_context(nc.sbuf_tensor(name, shape, dt))

        def ps(name, shape, dt=F32):
            return stack.enter_context(nc.psum_tensor(name, shape, dt))

        def sem(name):
            return stack.enter_context(nc.semaphore(name))

        x_sb = sb("x_sb", [128, B * QT, D])
        c_sb = sb("c_sb", [128, B * 4, D])
        aw = sb("aw", [128, 8, D])
        col = sb("col", [128, NCOLS])
        row = sb("row", [128, 2, D])
        rb_bc = sb("rb_bc", [128, E])
        w1_sb = sb("w1_sb", [128, 2, NC1, D])
        w1_hi = sb("w1_hi", [128, E, NC1, D], F32R)
        w1_lo = sb("w1_lo", [128, E, NC1, D], F32R)
        w2_sb = sb("w2_sb", [128, E, NC1, D])
        rw_sb = sb("rw_sb", [128, E])
        b2_sb = sb("b2_sb", [E, D])
        idf = sb("idf", [128, 128])
        idb = sb("idb", [128, 128], BF16)
        tri_sb = sb("tri_sb", [128, E, E])
        stats = sb("stats", [128, 4, 6])
        mv = sb("mv", [128, len(NORMS), 4, 2])
        veps = sb("veps", [128, len(NORMS), 4])
        rstd = sb("rstd", [128, len(NORMS), 4])
        mhalf = sb("mhalf", [128, 4])
        z_lat = sb("z_lat", [128, B * QT, D])
        zx = zy = z_lat
        zc = c_sb
        xT = sb("xT", [128, B, L])
        cT = sb("cT", [128, B, S])
        yT = wT = xT
        wT_hi = sb("wT_hi", [128, B, L], F32R)
        wT_lo = sb("wT_lo", [128, B, L], F32R)
        v_self = sb("v_self", [128, B, 2, H, DH + 1])
        v_cross = sb("v_cross", [128, B, 4, H, DH + 1])
        part_q = sb("part_q", [128, 2 * B, 3, 128], BF16)
        part_k = sb("part_k", [128, B, 3, S], BF16)
        rest = sb("rest", [128, L])
        rest_c = sb("rest_c", [128, S])
        q_op = sb("q_op", [128, 4, H, 128], BF16)
        k_self = sb("k_self", [128, B, H, L], BF16)
        k_cross = sb("k_cross", [128, B, H, S], BF16)
        negmax = sb("negmax", [128, 2, H])
        negmax_parts = sb("negmax_parts", [128, 2, 2, H], BF16)
        negmaxT = sb("negmaxT", [2 * H, 2, 128], BF16)
        probs = sb("probs", [128, NP_TILES, 512])
        av_sb = sb("av_sb", [128, 4, 128])
        rsum = sb("rsum", [128, H])
        attn = sb("attn", [128, D])
        attnT = sb("attnT", [128, 128])
        res = sb("res", [128, B * QT, D])
        x1 = sb("x1", [128, B * QT, D])
        res2 = res
        x2 = x1
        lg = sb("lg", [128, E])
        top = sb("top", [128, 1])
        above = sb("above", [128, E, E])
        ties = sb("ties", [128, E, E])
        rank = sb("rank", [128, E])
        shifted = sb("shifted", [128, E])
        ex = sb("ex", [128, E])
        den = sb("den", [128, 1])
        gates = sb("gates", [128, 2 * B, E])
        gatesT = sb("gatesT", [E, 2 * B, 128])
        warm = sb("warm", [128, 1])
        acc = x1

        s1 = ps("s1", [128, S1_BANKS, 512])
        s2 = ps("s2", [128, S2_BANKS, 512])
        avp = ps("avp", [128, 512])
        misc = ps("misc", [128, 2, 512])
        score_banks = [s1[:, k, :] for k in range(S1_BANKS)] + [s2[:, k, :] for k in range(S2_BANKS)]
        fc1_ring, fc2_ring = score_banks[0:4], [avp[:, :], score_banks[4]]

        scr_q = nc.dram_tensor("scr_q", [8, 3, D, 128], BF16, kind="Internal").ap()
        scr_ks = nc.dram_tensor("scr_ks", [B, 5, D, L], BF16, kind="Internal").ap()
        scr_kc = nc.dram_tensor("scr_kc", [B, 5, D, S], BF16, kind="Internal").ap()

        ld_x = [sem(f"ld_x{b}") for b in range(B)]
        ld_c = [sem(f"ld_c{b}") for b in range(B)]
        ld_aw, ld_aw2, ld_col, ld_row, ld_rb = sem("ld_aw"), sem("ld_aw2"), sem("ld_col"), sem("ld_row"), sem("ld_rb")
        ld_w1 = [sem(f"ld_w1_{e}") for e in range(E)]
        ld_w2, ld_rw, ld_b2 = sem("ld_w2"), sem("ld_rw"), sem("ld_b2")
        w1_hi_ready, w1_ready, wT_ready = sem("w1_hi_ready"), sem("w1_ready"), sem("wT_ready")
        ld_id, ld_tri = sem("ld_id"), sem("ld_tri")
        idb_ready, mhalf_ready, av_zero = sem("idb_ready"), sem("mhalf_ready"), sem("av_zero")
        v_ones = {"v": sem("v_self_ones"), "cv": sem("v_cross_ones")}
        q_wiped = [sem(f"q_wiped{u}") for u in range(4)]
        k_wiped = [sem(f"k_wiped{k}") for k in range(4)]
        var_ready, rstd_ready = sem("var_ready"), sem("rstd_ready")
        z_ready = {n: sem(f"z{n[0]}{n[1]}") for n in NORMS}
        misc_full = [sem(f"misc_full{k}") for k in range(2)]
        misc_read = [sem(f"misc_read{k}") for k in range(2)]
        hi_ready, mid_ready = sem("hi_ready"), sem("mid_ready")
        parts_ready = [sem(f"parts_ready{k}") for k in range(len(SPLITS))]
        k_stored = [sem(f"k_stored{k}") for k in range(len(SPLITS))]
        q_stored = [sem(f"q_stored{u}") for u in range(8)]
        q_second_half, k_second_half = sem("q_second_half"), sem("k_second_half")
        q_ready = [sem(f"q_ready{u}") for u in range(8)]
        k_ready = [sem(f"k_ready{k}") for k in range(4)]
        s1_full, s1_read = sem("s1_full"), sem("s1_read")
        negmax_ready = sem("negmax_ready")
        max_rows = [sem(f"max_rows{u}") for u in range(8)]
        s2_full, probs_ready = sem("s2_full"), sem("probs_ready")
        av_full, av_read = sem("av_full"), sem("av_read")
        res_ready, res2_ready = sem("res_ready"), sem("res2_ready")
        shifted_ready, ex_ready, gates_ready = sem("shifted_ready"), sem("ex_ready"), sem("gates_ready")
        fc1_full, gelu_ready, fc2_full, acc_step = sem("fc1_full"), sem("gelu_ready"), sem("fc2_full"), sem("acc_step")
        stored = sem("stored")
        dve_own = sem("dve_own")

        def bank(item):
            return MISC[item] % 2

        def wait_full(eng, item):
            eng.wait_ge(misc_full[bank(item)], MISC[item] // 2 + 1)

        def wait_free(eng, item):
            if MISC[item] // 2 > 0:
                eng.wait_ge(misc_read[bank(item)], MISC[item] // 2)

        def wait_read(eng, item):
            eng.wait_ge(misc_read[bank(item)], MISC[item] // 2 + 1)

        def parts_of(item):
            kind, idx = item
            if kind == "sk":
                return lambda m: m[:, 0:L], lambda t: part_k[:, idx, t, 0:L], SA_BK
            if kind == "sq":
                return (lambda m: m[:, 0:L].rearrange("p (t c) -> p t c", c=128),
                        lambda t: part_q[:, QT * idx:QT * (idx + 1), t, :], SA_BQ)
            if kind == "ck":
                return lambda m: m[:, 0:S], lambda t: part_k[:, idx, t, :], CA_BK
            return lambda m: m[:, 0:128], lambda t: part_q[:, idx, t, :], CA_BQ

        block = stack.enter_context(nc.Block())

        @block.sync
        def _(sp):
            tok = x.rearrange("(t p) d -> p t d", p=128)
            ctok = ctx_in.rearrange("(t p) d -> p t d", p=128)
            for b in range(B):
                sp.dma_start(x_sb[:, QT * b:QT * (b + 1), :], tok[:, QT * b:QT * (b + 1), :]).then_inc(ld_x[b], 16)
                if b == 0:
                    sp.dma_start(idf[:, :], ident).then_inc(ld_id, 16)
                    sp.dma_start(col[:, :], cols).then_inc(ld_col, 16)
                    sp.dma_start(aw[:, 0:4, :], attn_w[:, 0:4, :]).then_inc(ld_aw, 16)
            sp.dma_start(c_sb[:, 0:4, :], ctok[:, 0:4, :]).then_inc(ld_c[0], 16)
            sp.dma_start(row[:, :, :], rows.unsqueeze(0).broadcast_to([128, 2, D])).then_inc(ld_row, 16)
            sp.dma_start(aw[:, 4:8, :], attn_w[:, 4:8, :]).then_inc(ld_aw2, 16)
            experts_asked = 0

            def store(item):
                kind, idx = item
                j = SPLITS.index(item)
                sp.wait_ge(parts_ready[j], 1)
                if kind in ("sk", "ck"):
                    scr = scr_ks if kind == "sk" else scr_kc
                    for at, n in ((0, 3), (3, 2)):
                        sp.dma_start(scr[idx, at:at + n].rearrange("t p c -> p t c"),
                                     part_k[:, idx, 0:n, 0:scr.shape[-1]]).then_inc(k_stored[j], 16)
                else:
                    for u in units(item):
                        sp.dma_start(scr_q[u].rearrange("t p c -> p t c"), part_q[:, u % 4]).then_inc(q_stored[u], 16)

            def units(item):
                return (QT * item[1], QT * item[1] + 1) if item[0] == "sq" else (4 + item[1],)

            def fetch_k(item, heads, ready):
                kind, idx = item
                scr, op, blk = (scr_ks, k_self, idx) if kind == "sk" else (scr_kc, k_cross, 2 + idx)
                sp.wait_ge(k_stored[SPLITS.index(item)], 32)
                sp.wait_ge(k_wiped[blk], 1)
                rows = scr[idx].rearrange("t (d h) c -> (t d) (h c)", d=DH)
                n = rows.shape[1]
                part = n // H * len(heads)
                windows = bass.AP(rows.tensor, rows.offset + n // H * heads[0], [[DH * n, 3], [n, 3 * DH], [1, part]])
                sp.dma_start(op[0:MAXROW, idx, heads[0]:heads[-1] + 1, :], windows).then_inc(ready, 16)

            def fetch_q(u, heads, ready):
                sp.wait_ge(q_stored[u], 16)
                sp.wait_ge(q_wiped[u % 4], 1)
                src = scr_q[u].rearrange("t (d h) c -> (t d) (h c)", d=DH)[:, 128 * heads[0]:128 * (heads[-1] + 1)]
                sp.dma_start(q_op[0:MAXROW, u % 4, heads[0]:heads[-1] + 1, :],
                             src.unsqueeze(0).broadcast_to([3, 3 * DH, 128 * len(heads)])).then_inc(ready, 16)

            every = range(H)
            first, second = range(H // 2), range(H // 2, H)
            store(("sk", 0))
            store(("sq", 0))
            fetch_k(("sk", 0), first, k_ready[0])
            fetch_q(0, first, q_ready[0])
            fetch_k(("sk", 0), second, k_second_half)
            fetch_q(0, second, q_second_half)
            fetch_q(1, every, q_ready[1])
            store(("sk", 1))
            store(("sq", 1))
            fetch_k(("sk", 1), every, k_ready[1])
            fetch_q(2, every, q_ready[2])
            fetch_q(3, every, q_ready[3])
            sp.dma_start(c_sb[:, 4:8, :], ctok[:, 4:8, :]).then_inc(ld_c[1], 16)

            def set_max_rows(u):
                wait_read(sp, ("m", u))
                sp.dma_start(q_op[MAXROW:MAXROW + 2, u % 4, :, :], negmaxT[:, u % 2, :]).then_inc(max_rows[u], 16)

            for t in range(N_STEPS + B * E):
                for item in AFTER_SP[t]:
                    kind, (name, idx) = item
                    if kind == "rows":
                        set_max_rows(idx)
                    elif kind == "store":
                        store((name, idx))
                    else:
                        if name == "ck":
                            fetch_k((name, idx), every, k_ready[2 + idx])
                        else:
                            fetch_q(4 + idx, every, q_ready[4 + idx])
                        if (name, idx) == ("ck", 0):
                            sp.dma_start(rb_bc[:, :], rb.unsqueeze(0).broadcast_to([128, E])).then_inc(ld_rb, 16)
                            sp.dma_start(tri_sb[:, :, :], tri).then_inc(ld_tri, 16)
                            sp.dma_start(rw_sb[:, :], rw).then_inc(ld_rw, 16)
                            sp.dma_start(b2_sb[:, :], b2).then_inc(ld_b2, 16)
                        if name == "cq":
                            for e in range(2 * idx, 2 * idx + 2):
                                if e >= 2:
                                    sp.wait_ge(w1_ready, e - 1)
                                sp.dma_start(w1_sb[:, e % 2], w1[:, e]).then_inc(ld_w1[e], 16)
                                sp.dma_start(w2_sb[:, e], w2[:, e]).then_inc(ld_w2, 16)
            out_t = out.rearrange("(t p) d -> p t d", p=128)
            for b in range(B):
                sp.wait_ge(acc_step, E * (b + 1))
                sp.dma_start(out_t[:, QT * b:QT * (b + 1), :], acc[:, QT * b:QT * (b + 1), :]).then_inc(stored, 16)
            sp.wait_ge(stored, 16 * B)

        @block.gpsimd
        def _(pool):
            def power(n):
                w = NORM_TILES[NORMS[n][0]]
                pool.wait_ge(var_ready, n + 1)
                nc.gpsimd.tensor_tensor(rstd[:, n, 0:w], veps[:, n, 0:w], mhalf[:, 0:w], ALU.pow).then_inc(rstd_ready, 1)

            def norm_context(n):
                name = NORMS[n]
                power(n)
                pool.wait_ge(rstd_ready, n + 1)
                for t in range(4):
                    c = c_sb[:, 4 * name[1] + t, :]
                    last = nc.gpsimd.tensor_scalar(c, c, mv[:, n, t, 0:1], rstd[:, n, t:t + 1], ALU.subtract, ALU.mult)
                last.then_inc(z_ready[name], 1)

            def cut_w1(e):
                pool.wait_ge(ld_w1[e], 16)
                nc.gpsimd.tensor_scalar(w1_hi[:, e], w1_sb[:, e % 2], 1.0, 1.0, ALU.mult, ALU.mult).then_inc(w1_hi_ready, 1)
                pool.wait_ge(w1_hi_ready, e + 1)
                nc.gpsimd.tensor_tensor(w1_lo[:, e], w1_sb[:, e % 2], w1_hi[:, e].bitcast(F32), ALU.subtract
                                        ).then_inc(w1_ready, 1)

            def wipe_q(u):
                nc.gpsimd.memset(q_op[:, u].bitcast(F32), 0.0).then_inc(q_wiped[u], 1)

            def wipe_k(blk):
                k = k_self[:, blk] if blk < 2 else k_cross[:, blk - 2]
                nc.gpsimd.memset(k.bitcast(F32), ONES_PAIR).then_inc(k_wiped[blk], 1)

            nc.gpsimd.memset(mhalf[:, :], -0.5).then_inc(mhalf_ready, 1)
            wipe_k(0)
            pool.wait_ge(mhalf_ready, 1)
            power(0)
            power(1)
            wipe_q(1)
            nc.gpsimd.memset(v_self[:], 1.0).then_inc(v_ones["v"], 1)
            wipe_k(1)
            wipe_q(2)
            wipe_q(3)
            nc.gpsimd.memset(v_cross[:], 1.0).then_inc(v_ones["cv"], 1)
            for t in AFTER:
                for item in AFTER[t]:
                    kind, idx = item[0], item[1]
                    if kind == "cs":
                        norm_context(NORMS.index(("c", idx)))
                        if idx == 0:
                            wipe_k(2)
                            pool.wait_ge(ld_row, 16)
                            for b in range(B):
                                pool.wait_ge(ld_x[b], 16)
                            for q in range(B * QT):
                                last = nc.gpsimd.tensor_tensor(res[:, q, :], x_sb[:, q, :], row[:, SA_BO, :], ALU.add)
                            last.then_inc(res_ready, 1)
                            wipe_k(3)
                    elif kind == "cm":
                        pool.wait_ge(mid_ready, idx + 1)
                        nc.gpsimd.tensor_tensor(part_k[:, idx, 2, :], rest_c[:, :], part_k[:, idx, 1, :], ALU.subtract
                                                ).then_inc(parts_ready[SPLITS.index(("ck", idx))], 1)
                    elif kind == "op" and idx < 4:
                        power(NORMS.index(("y", idx)))
                        wait_read(pool, item)
                        nc.gpsimd.tensor_tensor(res2[:, idx, :], x1[:, idx, :], row[:, CA_BO, :], ALU.add
                                                ).then_inc(res2_ready, 1)
                        if idx:
                            cut_w1(2 * idx - 2)
                            cut_w1(2 * idx - 1)
                    elif kind == "op":
                        if idx == 4:
                            cut_w1(6)
                            cut_w1(7)
                        power(NORMS.index(("w", idx - 4)))

        @block.scalar
        def _(act):
            def identity(dst, src, bias, scale=1.0):
                return nc.scalar.activation(dst, src, ACT.Identity, bias=bias, scale=scale)

            def c(j):
                return col[:, j:j + 1]

            def extra(item):
                kind, idx = item[0], item[1]
                if kind == "ex":
                    act.wait_ge(shifted_ready, idx - 3)
                    nc.scalar.activation(ex[:, :], shifted[:, :], ACT.Exp).then_inc(ex_ready, 1)
                elif kind == "e":
                    gelus(idx)
                elif kind == "cm":
                    wait_read(act, ("ck", idx))
                    nc.scalar.copy(part_k[:, idx, 1, :], rest_c[:, :]).then_inc(mid_ready, 1)
                if kind in ("cs", "cm", "yn", "wn", "rt", "ex", "rg", "op", "oT", "b2", "e"):
                    return
                wait_full(act, item)
                m = misc[:, bank(item), :]
                free = misc_read[bank(item)]
                if kind == "xT":
                    identity(xT[:, idx, :], m[:, 0:L], c(SA_B), c(SA_G)).then_inc(free, 1)
                elif kind == "cT":
                    identity(cT[:, idx, :], m[:, 0:S], c(CKV_B), c(CKV_G)).then_inc(free, 1)
                elif kind == "yT":
                    b, at = idx // 2, 128 * (idx % 2)
                    identity(yT[:, b, at:at + 128], m[:, 0:128], c(CQ_B), c(CQ_G)).then_inc(free, 1)
                elif kind == "wT":
                    b, at = idx // 2 - 2, 128 * (idx % 2)
                    identity(wT_hi[:, b, at:at + 128], m[:, 0:128], c(MOE_B), c(MOE_G))
                    identity(wT[:, b, at:at + 128], m[:, 0:128], c(MOE_B), c(MOE_G)).then_inc(free, 1)
                elif kind in ("sk", "sq", "ck", "cq"):
                    if kind == "ck":
                        act.wait_ge(k_stored[SPLITS.index(("sk", idx))], 32)
                    elif kind == "cq":
                        act.wait_ge(q_stored[idx], 16)
                    view, part, bias = parts_of(item)
                    identity(part(0), view(m), c(bias)).then_inc(hi_ready, 1)
                elif kind in ("v", "cv"):
                    v, w = (v_self, 2) if kind == "v" else (v_cross, 4)
                    act.wait_ge(v_ones[kind], 1)
                    nc.scalar.copy(v[:, idx, :, :, 0:DH],
                                   m[:, 0:D * w].rearrange("p (t h d) -> p t h d", t=w, d=DH)).then_inc(free, 1)
                elif kind == "aT":
                    identity(attnT[:, :], m[:, 0:128], c(SA_BV if idx < 4 else CA_BV)).then_inc(free, 1)
                elif kind == "gT":
                    nc.scalar.copy(gatesT[:, idx - 4, :], m[0:E, 0:128]).then_inc(free, 1)
                elif kind == "m":
                    u = idx
                    if u >= 2:
                        act.wait_ge(max_rows[u - 2], 16)
                    nc.scalar.copy(negmaxT[:, u % 2, :], m.bitcast(BF16)[0:2 * H, 0:128]).then_inc(free, 1)

            def gelus(n):
                e = n % E
                for cp in range(2):
                    act.wait_ge(fc1_full, 2 * n + cp + 1)
                    if n >= 3 and cp == 0:
                        act.wait_ge(fc2_full, n - 2)
                    for q in range(2):
                        k = 2 * cp + q
                        last = nc.scalar.activation(
                            probs[:, 2 * (n % 3) + cp, L * q:L * (q + 1)], fc1_ring[(2 * n + cp) % 4][:, L * q:L * (q + 1)],
                            ACT.Gelu, bias=c(FC1_B + e * NC1 + k))
                    last.then_inc(gelu_ready, 1)

            act.wait_ge(mhalf_ready, 1)
            nc.scalar.activation(warm[:, :], mhalf[:, 0:1], ACT.Exp)
            act.wait_ge(ld_col, 16)
            for item in AFTER[-1]:
                extra(item)
            for t in range(N_STEPS + B * E):
                if pass2_at(t):
                    u, h = pass2_at(t)
                    if nbk(u) == 2 or h % 2:
                        n = BASE[u] + h * nbk(u) // 2
                        act.wait_ge(s2_full, n + 1)
                        if n >= NP_TILES:
                            old = n - NP_TILES
                            ou = max(q for q in range(8) if BASE[q] <= old)
                            act.wait_ge(av_full, 4 * ou + (old - BASE[ou]) // (2 * nbk(ou)) + 1)
                        nc.scalar.activation(probs[:, n % NP_TILES, :], score_banks[pass2_bank(n)], ACT.Exp,
                                             scale=SCALE).then_inc(probs_ready, 1)
                if av_at(t) and av_at(t)[1] == 3:
                    u = av_at(t)[0]
                    act.wait_ge(av_full, 4 * (u + 1))
                    if u:
                        wait_full(act, ("oT", u - 1))
                    nc.scalar.copy(av_sb[:, :, :], avp[:, :].rearrange("p (g c) -> p g c", c=128)).then_inc(av_read, 1)
                for item in AFTER[t]:
                    extra(item)

        @block.vector
        def _(dve):
            own = [0]

            def link(ins):
                own[0] += 1
                ins.then_inc(dve_own, 1)
                dve.wait_ge(dve_own, own[0])

            def norm_stats(name, src):
                n, w = NORMS.index(name), NORM_TILES[name[0]]
                for t in range(w):
                    last = nc.vector.bn_stats(stats[:, t, :], src[:, t, :])
                link(last)
                for t in range(w):
                    last = nc.vector.bn_aggr(mv[:, n, t, :], stats[:, t, :])
                link(last)
                nc.vector.tensor_scalar_add(veps[:, n, 0:w], mv[:, n, 0:w, 1], EPS).then_inc(var_ready, 1)

            def norm(name, src, z):
                n, w = NORMS.index(name), NORM_TILES[name[0]]
                dve.wait_ge(rstd_ready, n + 1)
                for t in range(w):
                    last = nc.vector.tensor_scalar(z[:, t, :], src[:, t, :], mv[:, n, t, 0:1], rstd[:, n, t:t + 1],
                                                   ALU.subtract, ALU.mult)
                last.then_inc(z_ready[name], 1)

            def negmax_split(u):
                dve.wait_ge(s1_read, BASE[u + 1])
                if u >= 2:
                    wait_full(dve, ("m", u - 2))
                link(nc.vector.tensor_copy(negmax_parts[:, u % 2, 0, :], negmax[:, u % 2]))
                nc.vector.tensor_tensor(negmax_parts[:, u % 2, 1, :], negmax[:, u % 2],
                                        negmax_parts[:, u % 2, 0, :], ALU.subtract).then_inc(negmax_ready, 1)

            def split(item):
                j = SPLITS.index(item)
                m = misc[:, bank(item), :]
                wait_full(dve, item)
                dve.wait_ge(hi_ready, j + 1)
                view, part, bias = parts_of(item)
                left = rest_c if item[0] == "ck" else rest
                if item == ("ck", 1):
                    dve.wait_ge(parts_ready[SPLITS.index(("ck", 0))], 1)
                nc.vector.scalar_tensor_tensor(view(left), view(m), col[:, bias:bias + 1], part(0),
                                               ALU.add, ALU.subtract).then_inc(misc_read[bank(item)], 1)
                if item[0] != "ck":
                    wait_read(dve, item)
                    link(nc.vector.tensor_copy(part(1), view(left)))
                    nc.vector.tensor_tensor(part(2), view(left), part(1), ALU.subtract).then_inc(parts_ready[j], 1)
                    dve.wait_ge(parts_ready[j], 1)

            def rank_logits(item):
                wait_full(dve, item)
                nc.vector.tensor_tensor(lg[:, :], misc[:, bank(item), 0:E], rb_bc[:, :], ALU.add
                                        ).then_inc(misc_read[bank(item)], 1)
                wait_read(dve, item)
                link(nc.vector.tensor_reduce(top[:, :], lg[:, :], AXX, ALU.max))
                nc.vector.tensor_scalar(shifted[:, :], lg[:, :], top[:, 0:1], None, ALU.subtract).then_inc(shifted_ready, 1)
                mine = lg[:, :].unsqueeze(2).broadcast_to([128, E, E])
                others = lg[:, :].unsqueeze(1).broadcast_to([128, E, E])
                link(nc.vector.tensor_tensor(ties[:, :, :], others, mine, ALU.is_equal))
                nc.vector.tensor_tensor(above[:, :, :], others, mine, ALU.is_gt)
                link(nc.vector.tensor_tensor(ties[:, :, :], ties[:, :, :], tri_sb[:, :, :], ALU.mult))
                link(nc.vector.tensor_tensor(above[:, :, :], above[:, :, :], ties[:, :, :], ALU.add))
                link(nc.vector.tensor_reduce(rank[:, :], above[:, :, :], AXX, ALU.add))

            def set_gates(u):
                dve.wait_ge(ex_ready, u - 3)
                link(nc.vector.scalar_tensor_tensor(rank[:, :], rank[:, :], 1.5, ex[:, :], ALU.is_lt, ALU.mult))
                link(nc.vector.tensor_reduce(den[:, :], rank[:, :], AXX, ALU.add))
                link(nc.vector.reciprocal(den[:, :], den[:, :]))
                nc.vector.tensor_scalar(gates[:, u - 4, :], rank[:, :], den[:, 0:1], None, ALU.mult).then_inc(gates_ready, 1)
                dve.wait_ge(gates_ready, u - 3)

            def add_expert(n):
                b, e = divmod(n, E)
                dve.wait_ge(fc2_full, n + 1)
                for q in range(QT):
                    t = QT * b + q
                    last = nc.vector.scalar_tensor_tensor(acc[:, t, :], fc2_ring[n % 2][:, D * q:D * (q + 1)],
                                                          gates[:, t, e:e + 1], acc[:, t, :], ALU.mult, ALU.add)
                last.then_inc(acc_step, 1)
                dve.wait_ge(acc_step, n + 1)

            def extra(item):
                kind, idx = item[0], item[1]
                if kind == "cs":
                    dve.wait_ge(ld_c[idx], 16)
                    norm_stats(("c", idx), c_sb[:, 4 * idx:4 * idx + 4, :])
                elif kind in ("sk", "sq", "ck", "cq"):
                    split(item)
                elif kind == "oT":
                    wait_full(dve, item)
                    o = misc[:, bank(item), :].rearrange("p (h c) -> p h c", c=32)
                    link(nc.vector.reciprocal(rsum[:, :], o[:, :, DH]))
                    if idx:
                        wait_full(dve, ("aT", idx - 1))
                    nc.vector.tensor_tensor(attn[:, :].rearrange("p (h d) -> p h d", d=DH), o[:, :, 0:DH],
                                            rsum[:, :].unsqueeze(2).broadcast_to([128, H, DH]),
                                            ALU.mult).then_inc(misc_read[bank(item)], 1)
                    wait_read(dve, item)
                elif kind == "op":
                    wait_full(dve, item)
                    t = idx % 4
                    if idx < 4:
                        dve.wait_ge(res_ready, 1)
                    else:
                        dve.wait_ge(res2_ready, t + 1)
                    nc.vector.tensor_tensor(x1[:, t, :], misc[:, bank(item), 0:128], res[:, t, :],
                                            ALU.add).then_inc(misc_read[bank(item)], 1)
                    wait_read(dve, item)
                    norm_stats(("y" if idx < 4 else "w", t), x1[:, t:t + 1, :])
                elif kind == "yn":
                    norm(("y", idx), x1[:, idx:idx + 1, :], zy[:, idx:idx + 1, :])
                elif kind == "wn":
                    t = idx - 4
                    norm(("w", t), x2[:, t:t + 1, :], zx[:, t:t + 1, :])
                elif kind == "wT":
                    wait_read(dve, item)
                    b, at = idx // 2 - 2, 128 * (idx % 2)
                    nc.vector.tensor_tensor(wT_lo[:, b, at:at + 128], wT[:, b, at:at + 128],
                                            wT_hi[:, b, at:at + 128].bitcast(F32), ALU.subtract).then_inc(wT_ready, 1)
                elif kind == "rt":
                    if idx == 4:
                        dve.wait_ge(ld_rb, 16)
                        dve.wait_ge(ld_tri, 16)
                    rank_logits(item)
                elif kind == "rg":
                    set_gates(idx)
                elif kind == "b2":
                    wait_full(dve, item)
                    t = idx - 4
                    nc.vector.tensor_tensor(acc[:, t, :], misc[:, bank(item), 0:D], x2[:, t, :],
                                            ALU.add).then_inc(misc_read[bank(item)], 1)
                    wait_read(dve, item)
                elif kind == "e" and idx:
                    add_expert(idx - 1)

            nc.vector.memset(q_op[:, 0].bitcast(F32), 0.0).then_inc(q_wiped[0], 1)
            nc.vector.memset(avp[:, :], 0.0).then_inc(av_zero, 1)
            for b in range(B):
                dve.wait_ge(ld_x[b], 16)
                norm_stats(("x", b), x_sb[:, QT * b:QT * (b + 1), :])
                if b == 0:
                    dve.wait_ge(ld_id, 16)
                    nc.vector.tensor_copy(idb[:, :], idf[:, :]).then_inc(idb_ready, 1)
                    norm(("x", b), x_sb[:, QT * b:QT * (b + 1), :], zx[:, QT * b:QT * (b + 1), :])
            norm(("x", 1), x_sb[:, QT:2 * QT, :], zx[:, QT:2 * QT, :])
            dve.wait_ge(ld_col, 16)
            for item in AFTER[-1]:
                extra(item)
            for t in range(N_STEPS + B * E):
                if pass1_at(t):
                    u, h = pass1_at(t)
                    n = BASE[u] + h * nbk(u) // 2
                    if nbk(u) == 2:
                        dve.wait_ge(s1_full, n + 1)
                        nc.vector.tensor_reduce(negmax[:, u % 2, h:h + 1], s1[:, n % S1_BANKS, :], AXX, ALU.max,
                                                negate=True).then_inc(s1_read, 1)
                    elif h % 2:
                        dve.wait_ge(s1_full, n + 1)
                        nc.vector.tensor_reduce(negmax[:, u % 2, h - 1:h + 1],
                                                s1[:, n % S1_BANKS, :].rearrange("p (h k) -> p h k", h=2), AXX, ALU.max,
                                                negate=True).then_inc(s1_read, 1)
                    if h == H - 1:
                        negmax_split(u)
                for item in AFTER_DVE[t]:
                    extra(item)
            add_expert(B * E - 1)

        @block.tensor
        def _(pe):
            def mm(dst, lhsT, rhs, start=True, stop=True):
                return nc.tensor.matmul(dst, lhsT, rhs, start=start, stop=stop)

            def extra(item):
                kind, idx = item[0], item[1]
                if kind in ("cs", "cm", "yn", "wn", "ex", "rg"):
                    return
                if kind == "e":
                    fc1(idx)
                    if idx:
                        fc2(idx - 1)
                    return
                m = misc[:, bank(item), :]
                wait_free(pe, item)
                if kind in ("xT", "cT", "yT", "wT"):
                    name = (kind[0], idx % 4 if kind == "wT" else idx)
                    z = zc if kind == "cT" else z_lat
                    w = NORM_TILES[kind[0]]
                    pe.wait_ge(z_ready[name], 1)
                    for t in range(w):
                        last = nc.tensor.transpose(m[:, 128 * t:128 * (t + 1)], z[:, w * name[1] + t, :], idf[:, :])
                elif kind in ("sk", "sq"):
                    wait_read(pe, ("xT", idx))
                    last = mm(m[:, 0:L], aw[:, SK if kind == "sk" else SQ, :], xT[:, idx, :])
                elif kind == "v":
                    for t in range(2):
                        last = mm(m[:, D * t:D * (t + 1)], xT[:, idx, 128 * t:128 * (t + 1)], aw[:, SV, :])
                elif kind == "ck":
                    pe.wait_ge(ld_aw2, 16)
                    wait_read(pe, ("cT", idx))
                    last = mm(m, aw[:, CK, :], cT[:, idx, :])
                elif kind == "cv":
                    for t in range(4):
                        last = mm(m[:, D * t:D * (t + 1)], cT[:, idx, 128 * t:128 * (t + 1)], aw[:, CV, :])
                elif kind == "cq":
                    wait_read(pe, ("yT", idx))
                    last = mm(m[:, 0:128], aw[:, CQ, :], yT[:, idx // 2, 128 * (idx % 2):128 * (idx % 2 + 1)])
                elif kind == "m":
                    pe.wait_ge(negmax_ready, idx + 1)
                    pe.wait_ge(idb_ready, 1)
                    last = nc.tensor.transpose(m.bitcast(BF16)[0:2 * H, 0:128],
                                               negmax_parts[:, idx % 2].rearrange("p a h -> p (a h)"), idb[:, :])
                elif kind == "oT":
                    pe.wait_ge(av_read, idx + 1)
                    for g in range(4):
                        last = nc.tensor.transpose(m[:, 128 * g:128 * (g + 1)], av_sb[:, g, :], idf[:, :])
                elif kind == "aT":
                    wait_read(pe, ("oT", idx))
                    last = nc.tensor.transpose(m[:, 0:128], attn[:, :], idf[:, :])
                elif kind == "op":
                    wait_read(pe, ("aT", idx))
                    last = mm(m[:, 0:D], attnT[:, :], aw[:, SO if idx < 4 else CO, :])
                elif kind == "rt":
                    pe.wait_ge(ld_rw, 16)
                    wait_read(pe, ("wT", idx))
                    last = mm(m[:, 0:E], wT[:, idx // 2 - 2, 128 * (idx % 2):128 * (idx % 2 + 1)], rw_sb[:, :])
                elif kind == "gT":
                    pe.wait_ge(gates_ready, idx - 3)
                    last = nc.tensor.transpose(m[0:E, 0:128], gates[:, idx - 4, :], idf[:, :])
                elif kind == "b2":
                    pe.wait_ge(ld_b2, 16)
                    wait_read(pe, ("gT", idx))
                    last = mm(m[:, 0:D], gatesT[:, idx - 4, :], b2_sb[:, :])
                last.then_inc(misc_full[bank(item)], 1)

            def keys(u):
                return k_self[:, u // 2] if u < 4 else k_cross[:, u // 2 - 2]

            def pass1(u, h):
                k = keys(u)
                if h == 0:
                    pe.wait_ge(q_ready[u], 16)
                    pe.wait_ge(k_ready[u // 2], 16)
                elif u == 0 and h == H // 2:
                    pe.wait_ge(q_second_half, 16)
                    pe.wait_ge(k_second_half, 16)
                n, at = BASE[u] + h * nbk(u) // 2, (L * (h % 2) if nbk(u) == 1 else 0)
                if n >= S1_BANKS and at == 0:
                    pe.wait_ge(s1_read, n - S1_BANKS + 1)
                last = mm(s1[:, n % S1_BANKS, at:at + k.shape[-1]], q_op[:, u % 4, h, :], k[:, h, :])
                if h % 2 or nbk(u) == 2:
                    last.then_inc(s1_full, 1)

            def pass2(u, h):
                k, chunks = keys(u), 2 * nbk(u)
                if h == 0:
                    pe.wait_ge(max_rows[u], 16)
                n = BASE[u] + h * nbk(u) // 2
                if h % 2 == 0 or nbk(u) == 2:
                    if last_in_bank(n) is not None:
                        pe.wait_ge(probs_ready, last_in_bank(n) + 1)
                    if pass2_bank(n) < S1_BANKS:
                        pe.wait_ge(s1_read, BASE[8])
                for kc in range(chunks):
                    at = 128 * ((h * chunks + kc) % 4)
                    last = mm(score_banks[pass2_bank(n)][:, at:at + 128], k[:, h, 128 * kc:128 * (kc + 1)],
                              q_op[:, u % 4, h, :])
                if h % 2 or nbk(u) == 2:
                    last.then_inc(s2_full, 1)

            def times_v(u, g):
                b, chunks = (u // 2) % 2, 2 * nbk(u)
                v = v_self[:, b] if u < 4 else v_cross[:, b]
                if g == 0:
                    wait_read(pe, ("v" if u < 4 else "cv", b))
                    if u:
                        pe.wait_ge(av_read, u)
                pe.wait_ge(probs_ready, BASE[u] + 2 * (g + 1) * nbk(u))
                for kc in range(chunks):
                    for j in range(4):
                        h = 4 * g + j
                        n = BASE[u] + (h * chunks + kc) // 4
                        at = 128 * ((h * chunks + kc) % 4)
                        last = mm(avp[32 * j:32 * j + DH + 1, 128 * g:128 * (g + 1)], v[:, kc, h, :],
                                  probs[:, n % NP_TILES, at:at + 128], start=kc == 0, stop=kc == chunks - 1)
                last.then_inc(av_full, 1)

            def fc1(n):
                b, e = divmod(n, E)
                if n == 0:
                    pe.wait_ge(w1_ready, E)
                if e == 0:
                    pe.wait_ge(wT_ready, QT * (b + 1))
                for cp in range(2):
                    f = 2 * n + cp
                    if f >= 4:
                        pe.wait_ge(gelu_ready, f - 3)
                    else:
                        pe.wait_ge(probs_ready, max(k for k in range(BASE[8]) if pass2_bank(k) == f) + 1)
                    for q in range(2):
                        k, dst = 2 * cp + q, fc1_ring[f % 4][:, L * q:L * (q + 1)]
                        mm(dst, w1_hi[:, e, k, :], wT_hi[:, b, :], stop=False)
                        mm(dst, w1_hi[:, e, k, :], wT_lo[:, b, :], start=False, stop=False)
                        last = mm(dst, w1_lo[:, e, k, :], wT_hi[:, b, :], start=False)
                    last.then_inc(fc1_full, 1)

            def fc2(n):
                b, e = divmod(n, E)
                if n == 0:
                    pe.wait_ge(av_read, 8)
                    pe.wait_ge(probs_ready, BASE[8])
                    pe.wait_ge(ld_w2, 16 * E)
                pe.wait_ge(gelu_ready, 2 * n + 2)
                if n >= 2:
                    pe.wait_ge(acc_step, n - 1)
                for q in range(QT):
                    for k in range(NC1):
                        hidden = probs[:, 2 * (n % 3) + k // 2, L * (k % 2) + 128 * q:L * (k % 2) + 128 * (q + 1)]
                        last = mm(fc2_ring[n % 2][:, D * q:D * (q + 1)], hidden, w2_sb[:, e, k, :],
                                  start=k == 0, stop=k == NC1 - 1)
                last.then_inc(fc2_full, 1)

            pe.wait_ge(ld_id, 16)
            pe.wait_ge(ld_aw, 16)
            pe.wait_ge(av_zero, 1)
            for item in AFTER[-1]:
                extra(item)
            for t in range(N_STEPS + B * E):
                if pass1_at(t):
                    pass1(*pass1_at(t))
                if pass2_at(t):
                    pass2(*pass2_at(t))
                if av_at(t):
                    times_v(*av_at(t))
                for item in AFTER[t]:
                    extra(item)
            fc2(B * E - 1)


def kernel(**inputs):
    import concourse.bacc as bacc
    from concourse.bass_utils import run_bass_kernel_spmd

    a = {k.replace("L0_xattn_", ""): np.asarray(v) for k, v in inputs.items()}
    order = np.arange(D).reshape(H, DH).T.reshape(D)

    def qkvo(in_w, out_w):
        wq, wk, wv = in_w[0:D], in_w[D:2 * D], in_w[2 * D:]
        return [wq[order].T, wk[order].T, wv.T, out_w.T]

    attn_w = np.stack(qkvo(a["sa_in_w"], a["sa_out_w"]) + qkvo(a["ca_in_w"], a["ca_out_w"]), axis=1)
    sab, cab = a["sa_in_b"], a["ca_in_b"]
    cols = np.stack([a["sa_ln_g"], a["sa_ln_b"], a["ca_q_ln_g"], a["ca_q_ln_b"], a["ca_kv_ln_g"], a["ca_kv_ln_b"],
                     a["moe_ln_g"], a["moe_ln_b"], sab[0:D][order], sab[D:2 * D][order],
                     cab[0:D][order], cab[D:2 * D][order], sab[2 * D:], cab[2 * D:],
                     *a["e_fc1_b"].reshape(E * NC1, D)], axis=1)
    rows = np.stack([a["sa_out_b"], a["ca_out_b"]])
    e = np.arange(E)
    host = {
        "x": a["x"].reshape(B * L, D),
        "ctx_in": a["ctx_1024"].reshape(B * S, D),
        "attn_w": attn_w,
        "cols": cols,
        "rows": rows,
        "rb": a["router_b"],
        "w1": a["e_fc1_w"].transpose(2, 0, 1).reshape(D, E, NC1, D),
        "w2": a["e_fc2_w"].reshape(E, D, NC1, D).transpose(3, 0, 2, 1),
        "rw": a["router_w"].T,
        "b2": a["e_fc2_b"],
        "ident": np.eye(128, dtype=np.float32),
        "tri": np.broadcast_to((e[None, :] < e[:, None]).astype(np.float32), (128, E, E)),
    }
    nc = bacc.Bacc("TRN2", target_bir_lowering=False, num_devices=1)
    arrays, args = {}, []
    for name, v in host.items():
        v = np.ascontiguousarray(v)
        arrays[name + "_dram"] = v
        args.append(nc.dram_tensor(name + "_dram", v.shape, mybir.dt.from_np(v.dtype), kind="ExternalInput").ap())
    out = nc.dram_tensor("out_dram", [B * L, D], F32, kind="ExternalOutput").ap()
    xattn_moe(nc, *args, out)
    r = run_bass_kernel_spmd(nc, [arrays], core_ids=[0])
    return r.results[0]["out_dram"].reshape(B, L, D)
```
